# Optimizing a Trainium2 kernel written in Bass

```python
import numpy as np
import jax
import jax.numpy as jnp

def _softmax(x, axis=-1):
    return jax.nn.softmax(x, axis=axis)

def _gelu(x):
    return jax.nn.gelu(x, approximate=True)

def _silu(x):
    return jax.nn.silu(x)

def _sigmoid(x):
    return jax.nn.sigmoid(x)

def _layernorm(x, axis=-1, eps=1e-05):
    m = jnp.mean(x, axis=axis, keepdims=True)
    v = jnp.var(x, axis=axis, keepdims=True)
    return (x - m) / jnp.sqrt(v + eps)

def _scatter_add(tgt, idx, src, axis=0):
    return tgt.at[idx].add(src)

def _segment_sum(src, seg, n):
    return jax.ops.segment_sum(src, seg, n)
kernel_name = 'mk_xattn_ffn_d1_seqx_r8_a5a2f4'

def setup_inputs(seed: int=0):
    np.random.seed(seed)
    _w = jnp.asarray

    def _rec_inputs():
        import jax
        import jax.numpy as jnp
        _rk = jax.random.key(seed)
        x = 7.22e-05 + 1 * jax.random.normal(jax.random.fold_in(_rk, 1), (4, 256, 256), jnp.float32)
        _lenS = 256 - jax.random.randint(jax.random.fold_in(_rk, 7), (4,), 0, max(1, 256 // 4) + 1, jnp.int32)
        _lenS2 = 512 - jax.random.randint(jax.random.fold_in(_rk, 8), (4,), 0, max(1, 512 // 4) + 1, jnp.int32)
        _ctx_512P = jax.random.normal(jax.random.fold_in(_rk, 11), (4, 16, 64), jnp.float32)
        _ctx_512c = jax.random.dirichlet(jax.random.fold_in(_rk, 511), 0.3 * jnp.ones((16,), jnp.float32), (4, 512))
        _ctx_512t = jnp.einsum('bsk,bkd->bsd', _ctx_512c, _ctx_512P)
        _ctx_512t = _ctx_512t * jax.lax.rsqrt(jnp.mean(jnp.square(_ctx_512t)) + 1e-12) * 0.953939
        ctx_512 = -0.000514642 + 1.00011 * (_ctx_512t + 0.3 * jax.random.normal(jax.random.fold_in(_rk, 611), (4, 512, 64), jnp.float32))
        return (x, ctx_512)
    x, ctx_512 = _rec_inputs()

    def _L0_xattn_setup():
        import jax, jax.numpy as jnp
        import numpy as np
        B, S, H, NH, L = (2, 256, 256, 16, 64)
        HD = H // NH
        key = jax.random.key(seed)
        k1, k2, k3, k4, k5 = jax.random.split(key, 5)
        scale = 0.02
        return {'q': jax.random.normal(k1, (B, S, H), dtype=jnp.float32), 'latent_kv': jax.random.normal(k2, (B, S, L), dtype=jnp.float32), 'Wq': jax.random.normal(k3, (H, H), dtype=jnp.float32) * scale, 'Wkv_expand': jax.random.normal(k4, (2 * H, L), dtype=jnp.float32) * scale, 'Wout': jax.random.normal(k5, (H, H), dtype=jnp.float32) * scale}
    _L0_xattn_all = _L0_xattn_setup()
    _L0_xattn_in = {k: v for k, v in _L0_xattn_all.items() if k in ('Wq', 'Wkv_expand', 'Wout')}
    del _L0_xattn_all

    def _L0_ffn_setup():
        import jax, jax.numpy as jnp
        import numpy as np
        B, S, H = (1, 256, 256)
        E, K, I = (16, 4, 176)
        IS = 352
        CAP = 128
        key = jax.random.key(seed)
        ks = jax.random.split(key, 8)
        sc = 0.02
        return {'hidden_states': jax.random.normal(ks[0], (B, S, H), jnp.float32), 'gate_w': jax.random.normal(ks[1], (E, H), jnp.float32) * sc, 'w_gate': jax.random.normal(ks[2], (E, H, I), jnp.float32) * sc, 'w_up': jax.random.normal(ks[3], (E, H, I), jnp.float32) * sc, 'w_down': jax.random.normal(ks[4], (E, I, H), jnp.float32) * sc, 'sw_gate': jax.random.normal(ks[5], (H, IS), jnp.float32) * sc, 'sw_up': jax.random.normal(ks[6], (H, IS), jnp.float32) * sc, 'sw_down': jax.random.normal(ks[7], (IS, H), jnp.float32) * sc}
    _L0_ffn_all = _L0_ffn_setup()
    _L0_ffn_in = {k: v for k, v in _L0_ffn_all.items() if k in ('gate_w', 'w_gate', 'w_up', 'w_down', 'sw_gate', 'sw_up', 'sw_down')}
    del _L0_ffn_all
    return {'x': x, 'ctx_512': ctx_512, 'L0_xattn_Wq': _L0_xattn_in['Wq'], 'L0_xattn_Wkv_expand': _L0_xattn_in['Wkv_expand'], 'L0_xattn_Wout': _L0_xattn_in['Wout'], 'L0_ffn_gate_w': _L0_ffn_in['gate_w'], 'L0_ffn_w_gate': _L0_ffn_in['w_gate'], 'L0_ffn_w_up': _L0_ffn_in['w_up'], 'L0_ffn_w_down': _L0_ffn_in['w_down'], 'L0_ffn_sw_gate': _L0_ffn_in['sw_gate'], 'L0_ffn_sw_up': _L0_ffn_in['sw_up'], 'L0_ffn_sw_down': _L0_ffn_in['sw_down']}

def reference(x, ctx_512, L0_xattn_Wq, L0_xattn_Wkv_expand, L0_xattn_Wout, L0_ffn_gate_w, L0_ffn_w_gate, L0_ffn_w_up, L0_ffn_w_down, L0_ffn_sw_gate, L0_ffn_sw_up, L0_ffn_sw_down):
    import jax
    import jax.numpy as jnp

    def _L0_xattn_ref(q, latent_kv, Wq, Wkv_expand, Wout):
        import jax, jax.numpy as jnp
        import numpy as np
        B, S, H, NH, L = (2, 256, 256, 16, 64)
        HD = H // NH
        b, sq, _ = q.shape
        sk = latent_kv.shape[1]
        qp = q @ Wq.T
        kv = latent_kv @ Wkv_expand.T
        k, v = jnp.split(kv, 2, axis=-1)
        qh = qp.reshape(b, sq, NH, HD).transpose(0, 2, 1, 3)
        kh = k.reshape(b, sk, NH, HD).transpose(0, 2, 1, 3)
        vh = v.reshape(b, sk, NH, HD).transpose(0, 2, 1, 3)
        inv_sqrt_d = 1.0 / jnp.sqrt(jnp.float32(HD))
        scores = jnp.einsum('bhqd,bhkd->bhqk', qh, kh) * inv_sqrt_d
        causal = jnp.tril(jnp.ones((sq, sk), dtype=bool))
        scores = jnp.where(causal, scores, jnp.finfo(scores.dtype).min)
        attn = jax.nn.softmax(scores, axis=-1)
        out = jnp.einsum('bhqk,bhkd->bhqd', attn, vh)
        out = out.transpose(0, 2, 1, 3).reshape(b, sq, H)
        return out @ Wout.T

    def _L0_ffn_ref(hidden_states, gate_w, w_gate, w_up, w_down, sw_gate, sw_up, sw_down):
        import jax, jax.numpy as jnp
        import numpy as np
        B, S, H = (1, 256, 256)
        E, K, I = (16, 4, 176)
        IS = 352
        CAP = 128
        b, s, h = hidden_states.shape
        x = hidden_states.reshape(-1, h)
        T = x.shape[0]
        scores = jax.nn.softmax(x @ gate_w.T, axis=-1)
        topk_w, topk_i = jax.lax.top_k(scores, K)
        topk_w = topk_w / (topk_w.sum(-1, keepdims=True) + 1e-20)
        flat_i = topk_i.reshape(-1)
        flat_w = topk_w.reshape(-1)
        order = jnp.argsort(flat_i)
        se = flat_i[order]
        counts = jax.ops.segment_sum(jnp.ones_like(flat_i), flat_i, num_segments=E)
        starts = jnp.cumsum(counts) - counts
        rank = jnp.arange(T * K) - starts[se]
        tok = order // K
        slot = jnp.where(rank < CAP, rank, CAP)
        buf = jnp.full((E, CAP + 1), T, dtype=jnp.int32).at[se, slot].set(tok)[:, :CAP]
        wbuf = jnp.zeros((E, CAP + 1), x.dtype).at[se, slot].set(flat_w[order])[:, :CAP]
        xpad = jnp.concatenate([x, jnp.zeros((1, h), x.dtype)], axis=0)
        xg = xpad[buf]
        gact = jax.nn.silu(jnp.einsum('ech,ehi->eci', xg, w_gate))
        mid = gact * jnp.einsum('ech,ehi->eci', xg, w_up)
        eout = jnp.einsum('eci,eih->ech', mid, w_down) * wbuf[..., None]
        y = jnp.zeros((T + 1, h), x.dtype).at[buf.reshape(-1)].add(eout.reshape(-1, h))[:T]
        shared = jax.nn.silu(x @ sw_gate) * (x @ sw_up) @ sw_down
        return (y + shared).reshape(b, s, h)
    x = x + _L0_xattn_ref(_layernorm(x, axis=-1), ctx_512, L0_xattn_Wq, L0_xattn_Wkv_expand, L0_xattn_Wout)
    x = x + _L0_ffn_ref(_layernorm(x, axis=-1), L0_ffn_gate_w, L0_ffn_w_gate, L0_ffn_w_up, L0_ffn_w_down, L0_ffn_sw_gate, L0_ffn_sw_up, L0_ffn_sw_down)
    return x

_drawn_inputs = setup_inputs


def setup_inputs(seed=0):
    import zlib

    import numpy as np

    out = dict(_drawn_inputs(seed))
    spreads = {}
    factors = {'L0_xattn_Wq': 8.0,
     'L0_ffn_gate_w': 8.0,
     'L0_ffn_w_gate': 8.0,
     'L0_ffn_w_up': 8.0,
     'L0_ffn_w_down': 8.0,
     'L0_ffn_sw_gate': 2.89,
     'L0_ffn_sw_up': 2.852,
     'L0_ffn_sw_down': 2.853}
    for name, (base, spread) in spreads.items():
        noise = np.random.default_rng([zlib.crc32(name.encode()), seed]).standard_normal(out[name].shape)
        drawn = base * np.exp(spread * noise) if base else spread * noise
        out[name] = jnp.asarray(drawn.astype(out[name].dtype))
    for name, factor in factors.items():
        out[name] = (out[name] * factor).astype(out[name].dtype)
    return out
```

```python
from contextlib import ExitStack

import concourse.bass as bass
from concourse import mybir
from concourse.alu_op_type import AluOpType as ALU

F32 = mybir.dt.float32
BF16 = mybir.dt.bfloat16
I32 = mybir.dt.int32
ACT = mybir.ActivationFunctionType
AX = mybir.AxisListType

P = 128
B, S, H = 4, 256, 256
NT = B * S // P
NH, HD = 16, 16
L = 64
HC = H // P
QT = S // P
GH = 4
NG = NH // GH
E, TOPK, I = 16, 4, 176
IC = 88
IS = 352
SC = ((0, 128), (128, 128), (256, 96))
CAP = 128
T = B * S
EG = 4
EPS = 1e-5
FLOOR = -87.33
NEG = -(2.0 ** 127)

Q_PARTS = ((0, 3), (1, 2), (2, 1))
K_PARTS = ((0, 1, 2), (0, 1), (0,))
SPLIT_ROWS = 6 * HD
SHIFT_ROWS = 3
ROWS = SPLIT_ROWS + SHIFT_ROWS


def misc_order():
    jobs = []

    def proj(b):
        jobs.extend([("k", b), ("v", b), ("x", b), ("q", b)])

    def ffn_in(b):
        jobs.extend([("x2", b), ("logits", b)])

    proj(0)
    proj(1)
    jobs.append(("shift", 0))
    proj(2)
    for b in range(B):
        for g in range(NG):
            if g == 2 and b > 0:
                ffn_in(b - 1)
        if b + 1 < B:
            jobs.append(("shift", b + 1))
        jobs.extend([("ot", b, 0), ("ot", b, 1), ("at", b), ("wo", b)])
        if b + 3 < B:
            proj(b + 3)
    jobs.append(("shared", 0))
    jobs.append(("shared", 1))
    ffn_in(B - 1)
    jobs.append(("shared", 2))
    jobs.append(("shared", 3))
    jobs.append(("rank",))
    for e in range(E):
        if e == 0:
            jobs.append(("slots", 0))
        if e % EG == 1 and e // EG + 1 < E // EG:
            jobs.append(("slots", e // EG + 1))
        jobs.append(("down", e))
    return jobs


MISC = misc_order()
MISC_BANKS = 3
MISC_NO = {job: n for n, job in enumerate(MISC)}


def build(nc, x, ctx_t, wq_t, wkv_t, wo_t, gate_t, w_gu, w_dn, sw_gu, sw_dn, out):
    q_parts_d = nc.dram_tensor("q_parts_d", [2, 3, H, S], BF16, kind="Internal").ap()
    k_parts_d = nc.dram_tensor("k_parts_d", [2, 3, H, S], BF16, kind="Internal").ap()
    xn2_d = nc.dram_tensor("xn2_d", [T + CAP, H], F32, kind="Internal").ap()
    acc_d = nc.dram_tensor("acc_d", [T + CAP, H], F32, kind="Internal").ap()

    with ExitStack() as ctx:
        def sb(name, shape, dt=F32):
            return ctx.enter_context(nc.sbuf_tensor(name, shape, dt))

        def sem(name):
            return ctx.enter_context(nc.semaphore(name))

        ident = sb("ident", [P, P])
        ident_b = sb("ident_b", [P, P], BF16)
        above_b = sb("above_b", [P, P], BF16)
        ones_b = sb("ones_b", [P, P], BF16)
        mask_b = sb("mask_b", [P, P], BF16)
        slot_iota = sb("slot_iota", [P, P], BF16)
        cst = sb("cst", [P, P])
        spare_row = sb("spare_row", [P, 1])
        eps = sb("eps", [P, 1])
        zero_rows = sb("zero_rows", [P, H])
        wq = sb("wq", [P, HC, H])
        wkv = sb("wkv", [L, 2 * H])
        wo = sb("wo", [P, HC, H])
        gate = sb("gate", [P, HC, E])
        sgu = sb("sgu", [P, HC, 2, IS])
        sdn = sb("sdn", [P, 3, H])
        wgu = sb("wgu", [P, 2, EG, HC, 2, I])
        wdn = sb("wdn", [IC, 2, EG, 2, H])
        lat = sb("lat", [L, B, S])
        xs = sb("xs", [P, NT, H])
        xn = sb("xn", [P, 2, QT, H])
        xn_t = sb("xn_t", [P, HC * S])
        stats = sb("stats", [P, NT, 6])
        mv = sb("mv", [P, NT, 2])
        std = sb("std", [P, NT])
        rstd = sb("rstd", [P, NT])
        parts = {k: sb(f"{k}_parts", [P, 2, 3, 2 * S], BF16) for k in "kq"}
        rest = sb("rest", [P, 2, 2 * S])
        q_rows = sb("q_rows", [P, 2, NH, S], BF16)
        k_rows = sb("k_rows", [P, 2, NH, S], BF16)
        v_ones = sb("v_ones", [P, 3, QT, NH, 2 * HD])
        top = sb("top", [P, 2, QT, NH])
        shift = sb("shift", [P, 2, QT, 3, NH], BF16)
        shift_rest = sb("shift_rest", [P, QT, NH])
        shift_t = sb("shift_t", [3 * NH, 2, S], BF16)
        probs = sb("probs", [P, 2, 3, 2 * S])
        o_t = sb("o_t", [P, NG, S])
        den = sb("den", [P, QT, NH])
        attn = sb("attn", [P, QT, NH, HD])
        attn_t = sb("attn_t", [P, HC * S])
        stats2 = sb("stats2", [P, NT, 6])
        mv2 = sb("mv2", [P, NT, 2])
        std2 = sb("std2", [P, NT])
        rstd2 = sb("rstd2", [P, NT])
        xn2 = sb("xn2", [P, 2, QT, H])
        xn2_t = sb("xn2_t", [P, HC, T])
        logits = sb("logits", [P, NT, E])
        score = sb("score", [P, NT, E])
        r1 = sb("r1", [P, NT])
        r2 = sb("r2", [P, NT])
        best = sb("best", [P, NT, 8])
        above4 = sb("above4", [P, NT, E])
        tied = sb("tied", [P, NT, E])
        PAD = 8
        run_a = sb("run_a", [P, NT, PAD + E])
        run_b = sb("run_b", [P, NT, PAD + E])
        chosen = sb("chosen", [P, NT, E])
        chosen_b = sb("chosen_b", [P, NT, E], BF16)
        weight = sb("weight", [P, NT, E])
        kept = sb("kept", [P, NT, E])
        slot = sb("slot", [P, NT, E])
        tok_vals = sb("tok_vals", [P, NT, E, 6], BF16)
        onehot = sb("onehot", [P, EG, NT, CAP], BF16)
        slot_vals = sb("slot_vals", [P, EG, 6])
        tok_f = sb("tok_f", [P, EG])
        empty = sb("empty", [P, EG])
        tok_i = sb("tok_i", [P, E], I32)
        slot_w = sb("slot_w", [P, E])
        s_act = sb("s_act", [P, 2, S])
        s_mid = sb("s_mid", [P, 3, S])
        xg = sb("xg", [P, 3, H])
        xg_t = sb("xg_t", [P, 2, HC, CAP])
        e_act = sb("e_act", [IC, 2, 2 * CAP])
        e_mid = sb("e_mid", [IC, 2, 2, CAP])
        y_rows = sb("y_rows", [P, 3, H])

        s_ps = [ctx.enter_context(nc.psum_tensor(f"s_ps{i}", [P, 512], F32)) for i in range(2)]
        t_ps = [ctx.enter_context(nc.psum_tensor(f"t_ps{i}", [P, 512], F32)) for i in range(2)]
        o_ps = ctx.enter_context(nc.psum_tensor("o_ps", [P, 512], F32))
        m_ps = [ctx.enter_context(nc.psum_tensor(f"m_ps{i}", [P, 512], F32)) for i in range(MISC_BANKS)]

        consts = sem("consts")
        pool_chain = sem("pool_chain")
        dve_chain = sem("dve_chain")
        x_in = [sem(f"x_in{b}") for b in range(B)]
        lat_in = sem("lat_in")
        wkv_in = sem("wkv_in")
        wq_in = sem("wq_in")
        wo_in = sem("wo_in")
        gate_in = sem("gate_in")
        sw_in = sem("sw_in")
        ew_in = [sem(f"ew_in{i}") for i in range(2)]
        var_ready = sem("var_ready")
        std_ready = sem("std_ready")
        xn_ready = sem("xn_ready")
        misc_ready = [sem(f"misc_ready{i}") for i in range(MISC_BANKS)]
        misc_free = [sem(f"misc_free{i}") for i in range(MISC_BANKS)]
        xn_t_ready = sem("xn_t_ready")
        lead_ready = sem("lead_ready")
        rest_ready = sem("rest_ready")
        mid_ready = sem("mid_ready")
        low_ready = sem("low_ready")
        stored = {k: sem(f"{k}_stored") for k in "kq"}
        rows_in = {k: [sem(f"{k}_rows_in{i}") for i in range(2)] for k in "kq"}
        shift_in = [sem(f"shift_in{i}") for i in range(2)]
        v_ready = sem("v_ready")
        s_ready = sem("s_ready")
        s_free = sem("s_free")
        shift_ready = sem("shift_ready")
        shift_t_ready = sem("shift_t_ready")
        t_ready = sem("t_ready")
        t_free = sem("t_free")
        probs_masked = sem("probs_masked")
        o_ready = sem("o_ready")
        o_free = sem("o_free")
        attn_ready = sem("attn_ready")
        attn_t_ready = sem("attn_t_ready")
        var2_ready = sem("var2_ready")
        std2_ready = sem("std2_ready")
        xn2_ready = sem("xn2_ready")
        xn2_stored = [sem(f"xn2_stored{i}") for i in range(2)]
        zeros_stored = sem("zeros_stored")
        xn2_t_ready = sem("xn2_t_ready")
        z_ready = sem("z_ready")
        exp_ready = sem("exp_ready")
        chosen_ready = sem("chosen_ready")
        vals_ready = sem("vals_ready")
        onehot_ready = sem("onehot_ready")
        onehot_used = sem("onehot_used")
        tok_ready = sem("tok_ready")
        gu_ready = sem("gu_ready")
        gu_free = sem("gu_free")
        act_ready = sem("act_ready")
        mid_done = sem("mid_done")
        acc_ready = sem("acc_ready")
        acc_stored = sem("acc_stored")
        gathered = [sem(f"gathered{i}") for i in range(3)]
        xgt_ready = sem("xgt_ready")
        xg_t_ready = sem("xg_t_ready")
        y_ready = sem("y_ready")
        scattered = sem("scattered")
        out_stored = sem("out_stored")

        NS = 3 * NG
        SHARED = len(SC)

        def misc(job):
            n = MISC_NO[job]
            return m_ps[n % MISC_BANKS]

        def misc_begin(pe, job):
            n = MISC_NO[job]
            if n >= MISC_BANKS:
                pe.wait_ge(misc_free[n % MISC_BANKS], n // MISC_BANKS)

        def misc_end(ins, job):
            ins.then_inc(misc_ready[MISC_NO[job] % MISC_BANKS], 1)

        def misc_wait(eng, job):
            n = MISC_NO[job]
            eng.wait_ge(misc_ready[n % MISC_BANKS], n // MISC_BANKS + 1)

        def misc_done(ins, job):
            ins.then_inc(misc_free[MISC_NO[job] % MISC_BANKS], 1)

        def misc_copied(eng, job):
            n = MISC_NO[job]
            eng.wait_ge(misc_free[n % MISC_BANKS], n // MISC_BANKS + 1)

        def gu_no(b, c):
            return SHARED * b + c

        def gu_of(e):
            return SHARED * B + e

        block = ctx.enter_context(nc.Block())

        @block.sync
        def _(sp):
            sp.dma_start(lat[:, 0, :], ctx_t[0, :, 0:S]).then_inc(lat_in, 16)
            sp.dma_start(wkv[:], wkv_t).then_inc(wkv_in, 16)
            sp.dma_start(xs[:, 0:QT, :], x[0].rearrange("(t p) c -> p t c", p=P)).then_inc(x_in[0], 16)
            sp.dma_start(wq[:], wq_t.rearrange("(c p) n -> p c n", p=P)).then_inc(wq_in, 16)
            sp.dma_start(xs[:, QT:2 * QT, :], x[1].rearrange("(t p) c -> p t c", p=P)).then_inc(x_in[1], 16)
            sp.dma_start(lat[:, 1:B, :], ctx_t[1:B, :, 0:S].rearrange("b l k -> l b k")).then_inc(lat_in, 16)
            for b in range(2, B):
                sp.dma_start(xs[:, QT * b:QT * b + QT, :],
                             x[b].rearrange("(t p) c -> p t c", p=P)).then_inc(x_in[b], 16)

            def store_parts(b):
                for n, (k, d) in enumerate((("k", k_parts_d), ("q", q_parts_d))):
                    sp.wait_ge(low_ready, 2 * b + n + 1)
                    sp.dma_start(d[b % 2].rearrange("a (m p) t -> p (a m) t", p=P),
                                 parts[k][:, b % 2].rearrange("p a (m t) -> p (a m) t", m=2)
                                 ).then_inc(stored[k], 16)

            def load_rows(b):
                if b >= 2:
                    sp.wait_ge(t_ready, NS * (b - 1))
                sp.wait_ge(stored["k"], 16 * (b + 1))
                src = k_parts_d[b % 2].rearrange("a (h d) t -> a d h t", d=HD)
                row = 0
                for group in K_PARTS:
                    for part in group:
                        sp.dma_start(k_rows[row:row + HD, b % 2], src[part]).then_inc(rows_in["k"][b % 2], 16)
                        row += HD
                sp.wait_ge(stored["q"], 16 * (b + 1))
                src = q_parts_d[b % 2].rearrange("a (h d) t -> a d h t", d=HD)
                row = 0
                for part, copies in Q_PARTS:
                    for _ in range(copies):
                        sp.dma_start(q_rows[row:row + HD, b % 2], src[part]).then_inc(rows_in["q"][b % 2], 16)
                        row += HD

            store_parts(0)
            load_rows(0)
            store_parts(1)
            load_rows(1)
            sp.dma_start(wo[:], wo_t.rearrange("(c p) n -> p c n", p=P)).then_inc(wo_in, 16)
            sp.dma_start(gate[:], gate_t.rearrange("(c p) n -> p c n", p=P)).then_inc(gate_in, 16)
            sp.dma_start(sgu[:], sw_gu.rearrange("(c p) g i -> p c g i", p=P)).then_inc(sw_in, 16)
            sp.dma_start(sdn[:, 0:2, :], sw_dn[0:2 * P].rearrange("(c p) n -> p c n", p=P)).then_inc(sw_in, 16)
            sp.dma_start(sdn[0:IS - 2 * P, 2, :], sw_dn[2 * P:IS]).then_inc(sw_in, 16)

            def load_experts(g):
                if g >= 2:
                    n = MISC_NO[("down", EG * (g - 1) - 1)]
                    sp.wait_ge(misc_ready[n % MISC_BANKS], n // MISC_BANKS + 1)
                sp.dma_start(wgu[:, g % 2], w_gu[:, EG * g:EG * g + EG]).then_inc(ew_in[g % 2], 16)
                sp.dma_start(wdn[:, g % 2], w_dn[:, EG * g:EG * g + EG]).then_inc(ew_in[g % 2], 16)

            store_parts(2)
            load_rows(2)
            load_experts(0)
            load_experts(1)
            for b in range(B):
                if b == 0:
                    store_parts(3)
                    load_rows(3)
                sp.wait_ge(xn2_ready, b + 1)
                sp.dma_start(xn2_d[S * b:S * b + S].rearrange("(t p) c -> p t c", p=P),
                             xn2[:, b % 2]).then_inc(xn2_stored[b % 2], 16)
            for b in range(B):
                sp.wait_ge(acc_ready, b + 1)
                sp.dma_start(acc_d[S * b:S * b + S].rearrange("(t p) c -> p t c", p=P),
                             xs[:, QT * b:QT * b + QT]).then_inc(acc_stored, 16)
            load_experts(2)
            load_experts(3)
            sp.wait_ge(scattered, 16 * E)
            sp.dma_start(out.rearrange("b s c -> (b s) c"), acc_d[0:T]).then_inc(out_stored, 16)
            sp.wait_ge(out_stored, 16)

        @block.gpsimd
        def _(pool):
            n_chain = [0]

            def link(ins):
                n_chain[0] += 1
                ins.then_inc(pool_chain, 1)
                pool.wait_ge(pool_chain, n_chain[0])

            n_const = [0]

            def constant(ins):
                n_const[0] += 1
                ins.then_inc(consts, 1)
                pool.wait_ge(consts, n_const[0])

            constant(nc.gpsimd.memset(eps[:], EPS))
            link(nc.gpsimd.memset(ident[:], 0.0))
            constant(nc.gpsimd.affine_select(out=ident[:], in_=ident[:], compare_op=ALU.not_equal, fill=1.0,
                                             base=0, pattern=[[-1, P]], channel_multiplier=1))
            constant(nc.gpsimd.tensor_copy(ident_b[:], ident[:]))
            link(nc.gpsimd.memset(cst[:], 0.0))
            link(nc.gpsimd.affine_select(out=cst[:], in_=cst[:], compare_op=ALU.is_ge, fill=NEG,
                                         base=0, pattern=[[-1, P]], channel_multiplier=1))
            constant(nc.gpsimd.tensor_copy(mask_b[:], cst[:]))
            link(nc.gpsimd.memset(v_ones[:, :, :, :, HD:], 1.0))
            constant(nc.gpsimd.memset(k_rows[SPLIT_ROWS:P].rearrange("r b h t -> r (b h t)").bitcast(F32),
                                      1.0 + 0x3F80 / 2 ** 23))
            constant(nc.gpsimd.memset(zero_rows[:], 0.0))
            pool.dma_start(xn2_d[T:T + CAP], zero_rows[:]).then_inc(zeros_stored, 16)
            pool.dma_start(acc_d[T:T + CAP], zero_rows[:]).then_inc(zeros_stored, 16)

            def last_parts(b):
                for n, k in enumerate("kq"):
                    pool.wait_ge(mid_ready, 2 * b + n + 1)
                    if b >= 2:
                        pool.wait_ge(stored[k], 16 * (b - 1))
                    nc.gpsimd.tensor_tensor(parts[k][:, b % 2, 2, :], rest[:, n, :], parts[k][:, b % 2, 1, :],
                                            ALU.subtract).then_inc(low_ready, 1)

            def causal(b, g):
                for u in range(3):
                    n = NS * b + 3 * g + u
                    pool.wait_ge(t_free, n + 1)
                    if u < 2:
                        v = probs[:, g % 2, u, :].rearrange("p (h q) -> p h q", h=2)[:, :, 0:P]
                    else:
                        v = probs[:, g % 2, u, :].rearrange("p (h q) -> p h q", h=GH)
                    nc.gpsimd.affine_select(out=v, in_=v, compare_op=ALU.is_ge, fill=0.0, base=0,
                                            pattern=[[0, v.shape[1]], [1, P]],
                                            channel_multiplier=-1).then_inc(probs_masked, 1)

            last_parts(0)
            last_parts(1)
            link(nc.gpsimd.memset(cst[:], 1.0))
            link(nc.gpsimd.tensor_copy(ones_b[:], cst[:]))
            link(nc.gpsimd.affine_select(out=cst[:], in_=cst[:], compare_op=ALU.is_gt, fill=0.0,
                                         base=0, pattern=[[1, P]], channel_multiplier=-1))
            link(nc.gpsimd.tensor_copy(above_b[:], cst[:]))
            link(nc.gpsimd.iota(cst[:], pattern=[[1, P]], base=1, channel_multiplier=0,
                                allow_small_or_imprecise_dtypes=True))
            link(nc.gpsimd.tensor_copy(slot_iota[:], cst[:]))
            link(nc.gpsimd.iota(spare_row[:], pattern=[[0, 1]], base=T, channel_multiplier=1,
                                allow_small_or_imprecise_dtypes=True))
            link(nc.gpsimd.iota(cst[:], pattern=[[0, P]], base=0, channel_multiplier=1,
                                allow_small_or_imprecise_dtypes=True))
            v = cst[:].rearrange("p (t e) -> p t e", t=NT)
            link(nc.gpsimd.tensor_copy(tok_vals[:, :, :, 0], v))
            link(nc.gpsimd.iota(v, pattern=[[P, NT], [0, E]], base=0, channel_multiplier=0,
                                allow_small_or_imprecise_dtypes=True))
            link(nc.gpsimd.tensor_copy(tok_vals[:, :, :, 1], v))
            link(nc.gpsimd.memset(cst[:], 1.0))
            link(nc.gpsimd.tensor_copy(tok_vals[:, :, :, 2], v))
            link(nc.gpsimd.memset(run_a[:], 0.0))
            constant(nc.gpsimd.memset(run_b[:], 0.0))
            last_parts(2)
            for b in range(B):
                for g in range(NG):
                    causal(b, g)
                if b == 0:
                    last_parts(3)

            def gather(e):
                if e == 0:
                    pool.wait_ge(xn2_stored[0], 32)
                    pool.wait_ge(xn2_stored[1], 32)
                    pool.wait_ge(zeros_stored, 32)
                if e % EG == 0:
                    pool.wait_ge(tok_ready, e // EG + 1)
                if e >= 3:
                    pool.wait_ge(xgt_ready, e - 2)
                nc.gpsimd.indirect_dma_start(
                    out=xg[:, e % 3, :], out_offset=None, in_=xn2_d[:, :],
                    in_offset=bass.IndirectOffsetOnAxis(ap=tok_i[:, e:e + 1], axis=0),
                ).then_inc(gathered[e % 3], 16)

            def scatter(e):
                pool.wait_ge(y_ready, e + 1)
                if e == 0:
                    pool.wait_ge(acc_stored, 16 * B)
                else:
                    pool.wait_ge(scattered, 16 * e)
                nc.gpsimd.indirect_dma_start(
                    out=acc_d[:, :], out_offset=bass.IndirectOffsetOnAxis(ap=tok_i[:, e:e + 1], axis=0),
                    in_=y_rows[:, e % 3, :], in_offset=None, compute_op=ALU.add,
                ).then_inc(scattered, 16)

            for e in range(3):
                gather(e)
            for e in range(E):
                if e + 3 < E:
                    gather(e + 3)
                scatter(e)

        @block.scalar
        def _(act):
            def sqrt_var(lo, hi, src, dst, done):
                nc.scalar.activation(dst[:, lo:hi], src[:, lo:hi, 1], ACT.Sqrt, bias=eps[:, 0:1]).then_inc(done, 1)

            def copy_k(b):
                misc_wait(act, ("k", b))
                if b >= 2:
                    act.wait_ge(stored["k"], 16 * (b - 1))
                nc.scalar.activation(parts["k"][:, b % 2, 0, :], misc(("k", b))[:], ACT.Copy).then_inc(lead_ready, 1)

            def copy_rest(b):
                misc_wait(act, ("v", b))
                if b >= 3:
                    act.wait_ge(o_ready, NG * (b - 2))
                misc_done(nc.scalar.activation(
                    v_ones[:, b % 3, :, :, 0:HD],
                    misc(("v", b))[:].rearrange("p (c h d) -> p c h d", c=QT, h=NH), ACT.Copy), ("v", b))
                misc_wait(act, ("x", b))
                if b >= 1:
                    n = MISC_NO[("q", b - 1)]
                    act.wait_ge(misc_ready[n % MISC_BANKS], n // MISC_BANKS + 1)
                misc_x = nc.scalar.activation(xn_t[:], misc(("x", b))[:], ACT.Copy)
                misc_done(misc_x, ("x", b))
                misc_wait(act, ("q", b))
                if b >= 2:
                    act.wait_ge(stored["q"], 16 * (b - 1))
                nc.scalar.activation(parts["q"][:, b % 2, 0, :], misc(("q", b))[:], ACT.Copy).then_inc(lead_ready, 1)

            def exps(b, g, u):
                n = NS * b + 3 * g + u
                act.wait_ge(t_ready, n + 1)
                if n >= 6:
                    act.wait_ge(o_ready, NG * b + g - 1)
                nc.scalar.activation(probs[:, g % 2, u, :], t_ps[n % 2][:], ACT.Exp,
                                     scale=HD ** -0.5).then_inc(t_free, 1)

            def copy_o(b, g):
                act.wait_ge(o_ready, NG * b + g + 1)
                if b >= 1 and g == 0:
                    misc_wait(act, ("ot", b - 1, 1))
                nc.scalar.activation(o_t[:, g, :], o_ps[:, 0:S], ACT.Copy).then_inc(o_free, 1)

            def send_shift(b):
                misc_wait(act, ("shift", b))
                if b >= 2:
                    act.wait_ge(shift_in[b % 2], 48 * (b // 2))
                misc_done(nc.scalar.activation(shift_t[:, b % 2, :], misc(("shift", b))[0:3 * NH, 0:S], ACT.Copy),
                          ("shift", b))
                misc_copied(act, ("shift", b))
                if b >= 2:
                    act.wait_ge(t_ready, NS * (b - 1))
                for r in range(3):
                    act.dma_start(q_rows[SPLIT_ROWS + r:SPLIT_ROWS + r + 1, b % 2],
                                  shift_t[NH * r:NH * r + NH, b % 2, :]).then_inc(shift_in[b % 2], 16)

            def copy_at(b):
                misc_wait(act, ("at", b))
                if b >= 1:
                    misc_wait(act, ("wo", b - 1))
                misc_done(nc.scalar.activation(attn_t[:], misc(("at", b))[:], ACT.Copy), ("at", b))

            def copy_x2(b):
                misc_wait(act, ("x2", b))
                misc_done(nc.scalar.activation(
                    xn2_t[:, :, S * b:S * b + S],
                    misc(("x2", b))[:].rearrange("p (c t) -> p c t", c=HC), ACT.Copy), ("x2", b))

            def std2_of(b):
                act.wait_ge(var2_ready, b + 1)
                sqrt_var(QT * b, QT * b + QT, mv2, std2, std2_ready)

            def shared(b):
                for c, (_, size) in enumerate(SC):
                    n = gu_no(b, c)
                    act.wait_ge(gu_ready, n + 1)
                    if n >= 2:
                        act.wait_ge(mid_done, n - 1)
                    nc.scalar.activation(s_act[0:size, n % 2, :], s_ps[n % 2][0:size, 0:S],
                                         ACT.Silu).then_inc(act_ready, 1)

            act.wait_ge(consts, 1)
            act.wait_ge(var_ready, 1)
            sqrt_var(0, QT, mv, std, std_ready)
            copy_k(0)
            act.wait_ge(var_ready, B)
            sqrt_var(QT, NT, mv, std, std_ready)
            copy_rest(0)
            copy_k(1)
            copy_rest(1)
            send_shift(0)
            copy_k(2)
            copy_rest(2)
            for b in range(B):
                for g in range(NG):
                    for u in range(3):
                        exps(b, g, u)
                    if g >= 1:
                        copy_o(b, g - 1)
                    if g == 1 and b >= 1:
                        std2_of(b - 1)
                    if g == 2 and b >= 1:
                        copy_x2(b - 1)
                copy_o(b, NG - 1)
                if b + 1 < B:
                    send_shift(b + 1)
                copy_at(b)
                if b + 3 < B:
                    copy_k(b + 3)
                    copy_rest(b + 3)
            std2_of(B - 1)
            shared(0)
            shared(1)
            copy_x2(B - 1)
            act.wait_ge(z_ready, 1)
            nc.scalar.activation(score[:], logits[:], ACT.Exp).then_inc(exp_ready, 1)
            shared(2)
            shared(3)
            for e in range(E + 1):
                if e < E:
                    act.wait_ge(xgt_ready, e + 1)
                    if e >= 2:
                        act.wait_ge(gu_ready, gu_of(e - 2) + 1)
                    nc.scalar.activation(xg_t[:, e % 2].rearrange("p c s -> p (c s)"), t_ps[e % 2][:, 0:HC * CAP],
                                         ACT.Copy).then_inc(xg_t_ready, 1)
                if e >= 1:
                    n = gu_of(e - 1)
                    act.wait_ge(gu_ready, n + 1)
                    act.wait_ge(mid_done, n - 1)
                    nc.scalar.activation(e_act[:, n % 2, :], s_ps[n % 2][0:IC, 0:2 * CAP],
                                         ACT.Silu).then_inc(act_ready, 1)

        @block.vector
        def _(dve):
            n_chain = [0]

            def link(ins):
                n_chain[0] += 1
                ins.then_inc(dve_chain, 1)
                dve.wait_ge(dve_chain, n_chain[0])

            def wide(v, n):
                return v.unsqueeze(2).to_broadcast([P, v.shape[1], n])

            def norm_stats(src, b, st, m, done):
                for t in range(QT * b, QT * b + QT):
                    ins = nc.vector.bn_stats(out=st[:, t, :], in_=src[:, t, :])
                    if t % QT < QT - 1:
                        n_chain[0] += 1
                        ins.then_inc(dve_chain, 1)
                    else:
                        link(ins)
                for t in range(QT * b, QT * b + QT):
                    ins = nc.vector.bn_aggr(out=m[:, t, :], in_=st[:, t, :])
                    if t % QT < QT - 1:
                        link(ins)
                ins.then_inc(done, 1)

            def normalise(b):
                if b == 0:
                    dve.wait_ge(std_ready, 1)
                    link(nc.vector.reciprocal(rstd[:, 0:QT], std[:, 0:QT]))
                if b == 1:
                    dve.wait_ge(std_ready, 2)
                    link(nc.vector.reciprocal(rstd[:, QT:NT], std[:, QT:NT]))
                if b >= 2:
                    misc_wait(dve, ("x", b - 2))
                for t in range(QT):
                    k = QT * b + t
                    ins = nc.vector.tensor_scalar(xn[:, b % 2, t, :], xs[:, k, :], mv[:, k, 0:1], rstd[:, k:k + 1],
                                                  ALU.subtract, ALU.mult)
                    ins.then_inc(xn_ready, 1)

            def split(b, n, k):
                job = (k, b)
                dve.wait_ge(lead_ready, 2 * b + n + 1)
                if b >= 1:
                    dve.wait_ge(low_ready, 2 * (b - 1) + n + 1)
                misc_done(nc.vector.tensor_tensor(rest[:, n, :], misc(job)[:], parts[k][:, b % 2, 0, :],
                                                  ALU.subtract), job)
                misc_copied(dve, job)
                nc.vector.tensor_copy(parts[k][:, b % 2, 1, :], rest[:, n, :]).then_inc(mid_ready, 1)

            def maxima(b, u):
                n = NS * b + u
                dve.wait_ge(s_ready, n + 1)
                if u < 4:
                    src = s_ps[n % 2][:].rearrange("p (h k) -> p h k", h=GH)
                    dst = top[:, b % 2, 0, GH * u:GH * u + GH]
                else:
                    src = s_ps[n % 2][:].rearrange("p (h k) -> p h k", h=2)
                    dst = top[:, b % 2, 1, 2 * (u - 4):2 * (u - 4) + 2]
                nc.vector.tensor_reduce(dst, src, AX.X, ALU.max).then_inc(s_free, 1)

            def shift_parts(b):
                dve.wait_ge(s_free, NS * (b + 1))
                m, sh = top[:, b % 2], shift[:, b % 2]
                if b >= 2:
                    misc_wait(dve, ("shift", b - 2))
                link(nc.vector.tensor_scalar(sh[:, :, 0, :], m, -1.0, None, ALU.mult))
                link(nc.vector.scalar_tensor_tensor(out=shift_rest[:], in0=m, scalar=-1.0, in1=sh[:, :, 0, :],
                                                    op0=ALU.mult, op1=ALU.subtract))
                link(nc.vector.tensor_copy(sh[:, :, 1, :], shift_rest[:]))
                nc.vector.tensor_tensor(sh[:, :, 2, :], shift_rest[:], sh[:, :, 1, :],
                                        ALU.subtract).then_inc(shift_ready, 1)

            def attention_out(b, qt):
                job = ("ot", b, qt)
                misc_wait(dve, job)
                v = misc(job)[:].rearrange("p (h r) -> p h r", h=NH)
                link(nc.vector.reciprocal(den[:, qt, :], v[:, :, HD]))
                if b >= 1:
                    misc_wait(dve, ("at", b - 1))
                misc_done(nc.vector.tensor_tensor(attn[:, qt], v[:, :, 0:HD], wide(den[:, qt, :], HD), ALU.mult), job)

            def add_residual(b):
                job = ("wo", b)
                misc_wait(dve, job)
                v = xs[:, QT * b:QT * b + QT, :]
                misc_done(nc.vector.tensor_tensor(v, misc(job)[:].rearrange("p (t c) -> p t c", t=QT), v, ALU.add), job)
                misc_copied(dve, job)
                norm_stats(xs, b, stats2, mv2, var2_ready)

            def normalise2(b):
                dve.wait_ge(std2_ready, b + 1)
                link(nc.vector.reciprocal(rstd2[:, QT * b:QT * b + QT], std2[:, QT * b:QT * b + QT]))
                if b >= 2:
                    dve.wait_ge(xn2_stored[b % 2], 16 * (b // 2))
                    misc_wait(dve, ("x2", b - 2))
                for t in range(QT):
                    k = QT * b + t
                    ins = nc.vector.tensor_scalar(xn2[:, b % 2, t, :], xs[:, k, :], mv2[:, k, 0:1],
                                                  rstd2[:, k:k + 1], ALU.subtract, ALU.mult)
                    if t < QT - 1:
                        link(ins)
                ins.then_inc(xn2_ready, 1)

            def copy_logits(b):
                job = ("logits", b)
                misc_wait(dve, job)
                misc_done(nc.vector.tensor_copy(logits[:, QT * b:QT * b + QT, :],
                                                misc(job)[:, 0:QT * E].rearrange("p (t e) -> p t e", t=QT)), job)

            def shared_mid(b):
                for c, (_, size) in enumerate(SC):
                    n = gu_no(b, c)
                    dve.wait_ge(act_ready, n + 1)
                    if b >= 1 and c == 0:
                        misc_wait(dve, ("shared", b - 1))
                    nc.vector.tensor_tensor(s_mid[0:size, c, :], s_ps[n % 2][0:size, S:2 * S],
                                            s_act[0:size, n % 2, :], ALU.mult).then_inc(mid_done, 1)

            def shared_out(b):
                job = ("shared", b)
                misc_wait(dve, job)
                v = xs[:, QT * b:QT * b + QT, :]
                misc_done(nc.vector.tensor_tensor(v, misc(job)[:].rearrange("p (t c) -> p t c", t=QT), v, ALU.add), job)
                misc_copied(dve, job)
                dve.sem_inc(acc_ready, 1)

            def route_start():
                for b in range(B):
                    misc_copied(dve, ("logits", b))
                link(nc.vector.tensor_reduce(r1[:], logits[:], AX.X, ALU.max))
                nc.vector.tensor_tensor(logits[:], logits[:], wide(r1[:], E), ALU.subtract).then_inc(z_ready, 1)
                dve.wait_ge(z_ready, 1)
                link(nc.vector.tensor_scalar(above4[:], logits[:], FLOOR, None, ALU.max))
                for t in range(NT):
                    ins = nc.vector.max(out=best[:, t, :], in_=above4[:, t, :])
                    n_chain[0] += 1
                    ins.then_inc(dve_chain, 1)
                dve.wait_ge(dve_chain, n_chain[0])
                dve.wait_ge(consts, 7)
                fourth = wide(best[:, :, TOPK - 1], E)
                link(nc.vector.tensor_tensor(run_a[:, :, PAD:], above4[:], fourth, ALU.is_equal))
                link(nc.vector.tensor_copy(tied[:], run_a[:, :, PAD:]))
                link(nc.vector.tensor_tensor(above4[:], above4[:], fourth, ALU.is_gt))
                link(nc.vector.tensor_reduce(r1[:], above4[:], AX.X, ALU.add))
                src, dst = run_a, run_b
                for step in (1, 2, 4, 8):
                    link(nc.vector.tensor_tensor(dst[:, :, PAD:], src[:, :, PAD:],
                                                 src[:, :, PAD - step:PAD + E - step], ALU.add))
                    src, dst = dst, src
                link(nc.vector.tensor_tensor(chosen[:], src[:, :, PAD:], wide(r1[:], E), ALU.add))
                link(nc.vector.scalar_tensor_tensor(out=chosen[:], in0=chosen[:], scalar=float(TOPK), in1=tied[:],
                                                    op0=ALU.is_le, op1=ALU.mult))
                link(nc.vector.tensor_tensor(chosen[:], chosen[:], above4[:], ALU.add))
                nc.vector.tensor_copy(chosen_b[:], chosen[:]).then_inc(chosen_ready, 1)

            def route_weights():
                dve.wait_ge(exp_ready, 1)
                link(nc.vector.tensor_reduce(r1[:], score[:], AX.X, ALU.add))
                link(nc.vector.reciprocal(r2[:], r1[:]))
                link(nc.vector.tensor_tensor(score[:], score[:], wide(r2[:], E), ALU.mult))
                link(nc.vector.tensor_tensor(score[:], score[:], chosen[:], ALU.mult))
                link(nc.vector.tensor_reduce(r1[:], score[:], AX.X, ALU.add))
                link(nc.vector.tensor_scalar(r1[:], r1[:], 1e-20, None, ALU.add))
                link(nc.vector.reciprocal(r2[:], r1[:]))
                link(nc.vector.tensor_tensor(weight[:], score[:], wide(r2[:], E), ALU.mult))
                link(nc.vector.tensor_copy(tok_vals[:, :, :, 3], weight[:]))
                link(nc.vector.tensor_tensor(weight[:], weight[:], tok_vals[:, :, :, 3], ALU.subtract))
                link(nc.vector.tensor_copy(tok_vals[:, :, :, 4], weight[:]))
                nc.vector.tensor_tensor(tok_vals[:, :, :, 5], weight[:], tok_vals[:, :, :, 4],
                                        ALU.subtract).then_inc(vals_ready, 1)

            def slots_of_tokens():
                job = ("rank",)
                misc_wait(dve, job)
                rank = misc(job)[:, 0:NT * E].rearrange("p (t e) -> p t e", t=NT)
                link(nc.vector.scalar_tensor_tensor(out=kept[:], in0=rank, scalar=float(CAP), in1=chosen[:],
                                                    op0=ALU.is_lt, op1=ALU.mult))
                misc_done(nc.vector.scalar_tensor_tensor(out=slot[:], in0=rank, scalar=1.0, in1=kept[:],
                                                         op0=ALU.add, op1=ALU.mult), job)
                misc_copied(dve, job)

            def onehots(g):
                for e in range(EG * g, EG * g + EG):
                    if e >= EG:
                        dve.wait_ge(onehot_used, e - EG + 1)
                    for t in range(NT):
                        ins = nc.vector.tensor_scalar(onehot[:, e % EG, t, :], slot_iota[:], slot[:, t, e:e + 1],
                                                      None, ALU.is_equal)
                    ins.then_inc(onehot_ready, 1)

            def tokens_of_slots(g):
                job = ("slots", g)
                misc_wait(dve, job)
                misc_done(nc.vector.tensor_copy(slot_vals[:].rearrange("p e v -> p (e v)"), misc(job)[:, 0:EG * 6]), job)
                misc_copied(dve, job)
                link(nc.vector.tensor_tensor(tok_f[:], slot_vals[:, :, 0], slot_vals[:, :, 1], ALU.add))
                link(nc.vector.tensor_scalar(empty[:], slot_vals[:, :, 2], -1.0, 1.0, ALU.mult, ALU.add))
                link(nc.vector.tensor_reduce(slot_w[:, EG * g:EG * g + EG], slot_vals[:, :, 3:6], AX.X, ALU.add))
                nc.vector.scalar_tensor_tensor(out=tok_i[:, EG * g:EG * g + EG], in0=empty[:],
                                               scalar=spare_row[:, 0:1], in1=tok_f[:],
                                               op0=ALU.mult, op1=ALU.add).then_inc(tok_ready, 1)

            def expert_mid(e):
                n = gu_of(e)
                dve.wait_ge(act_ready, n + 1)
                if e >= 2:
                    misc_wait(dve, ("down", e - 2))
                nc.vector.tensor_tensor(e_mid[:, e % 2].rearrange("p c s -> p (c s)"), s_ps[n % 2][0:IC, 2 * CAP:],
                                        e_act[:, n % 2, :], ALU.mult).then_inc(mid_done, 1)

            def expert_out(e):
                job = ("down", e)
                misc_wait(dve, job)
                if e >= 3:
                    dve.wait_ge(scattered, 16 * (e - 2))
                misc_done(nc.vector.tensor_scalar(y_rows[:, e % 3, :], misc(job)[:, 0:H], slot_w[:, e:e + 1], None,
                                                  ALU.mult), job)
                misc_copied(dve, job)
                dve.sem_inc(y_ready, 1)

            for b in range(B):
                dve.wait_ge(x_in[b], 16)
                norm_stats(xs, b, stats, mv, var_ready)
                if b == 0:
                    normalise(0)
                    split(0, 0, "k")
            split(0, 1, "q")
            normalise(1)
            split(1, 0, "k")
            split(1, 1, "q")
            for u in range(NS):
                maxima(0, u)
            shift_parts(0)
            normalise(2)
            split(2, 0, "k")
            split(2, 1, "q")
            for b in range(B):
                for g in range(NG):
                    if b + 1 < B:
                        for u in range(3):
                            maxima(b + 1, 3 * g + u)
                    if g == 1 and b >= 1:
                        normalise2(b - 1)
                    if g == 2 and b >= 1:
                        copy_logits(b - 1)
                if b + 1 < B:
                    shift_parts(b + 1)
                attention_out(b, 0)
                attention_out(b, 1)
                if b + 3 < B:
                    normalise(b + 3)
                add_residual(b)
                if b + 3 < B:
                    split(b + 3, 0, "k")
                    split(b + 3, 1, "q")
            normalise2(B - 1)
            shared_mid(0)
            shared_out(0)
            shared_mid(1)
            copy_logits(B - 1)
            route_start()
            shared_out(1)
            shared_mid(2)
            shared_out(2)
            route_weights()
            shared_mid(3)
            slots_of_tokens()
            onehots(0)
            shared_out(3)
            tokens_of_slots(0)
            for e in range(E):
                if e % EG == 0 and e // EG + 1 < E // EG:
                    onehots(e // EG + 1)
                expert_mid(e)
                if e % EG == 1 and e // EG + 1 < E // EG:
                    tokens_of_slots(e // EG + 1)
                expert_out(e)

        @block.tensor
        def _(pe):
            def keys_values(b):
                if b == 0:
                    pe.wait_ge(lat_in, 16)
                    pe.wait_ge(wkv_in, 16)
                if b == 1:
                    pe.wait_ge(lat_in, 32)
                job = ("k", b)
                misc_begin(pe, job)
                for m in range(2):
                    last = nc.tensor.matmul(misc(job)[:, S * m:S * m + S], wkv[:, P * m:P * m + P], lat[:, b, :],
                                            start=True, stop=True)
                misc_end(last, job)
                job = ("v", b)
                misc_begin(pe, job)
                for c in range(QT):
                    last = nc.tensor.matmul(misc(job)[:, H * c:H * c + H], lat[:, b, P * c:P * c + P], wkv[:, H:],
                                            start=True, stop=True)
                misc_end(last, job)

            def queries(b):
                job = ("x", b)
                pe.wait_ge(xn_ready, QT * (b + 1))
                if b == 0:
                    pe.wait_ge(consts, 2)
                misc_begin(pe, job)
                for c in range(HC):
                    for t in range(QT):
                        o = S * c + P * t
                        last = nc.tensor.transpose(misc(job)[:, o:o + P], xn[:, b % 2, t, P * c:P * c + P], ident[:])
                misc_end(last, job)
                misc_copied(pe, job)
                if b == 0:
                    pe.wait_ge(wq_in, 16)
                job = ("q", b)
                misc_begin(pe, job)
                for m in range(2):
                    for c in range(HC):
                        last = nc.tensor.matmul(misc(job)[:, S * m:S * m + S], wq[:, c, P * m:P * m + P],
                                                xn_t[:, S * c:S * c + S], start=(c == 0), stop=(c == HC - 1))
                misc_end(last, job)

            def scores(b, u):
                n = NS * b + u
                if u == 0:
                    if b == 0:
                        pe.wait_ge(consts, 5)
                    for k in "kq":
                        pe.wait_ge(rows_in[k][b % 2], 16 * 6 * (b // 2 + 1))
                if n >= 2:
                    pe.wait_ge(s_free, n - 1)
                bank = s_ps[n % 2]
                if u < 4:
                    qt, heads, keys = 0, range(GH * u, GH * u + GH), P
                    masked = bank[:].rearrange("p (h k) -> p h k", h=GH)
                else:
                    qt, heads, keys = 1, range(2 * (u - 4), 2 * (u - 4) + 2), S
                    masked = bank[:].rearrange("p (h k) -> p h k", h=2)[:, :, P:]
                nc.tensor.matmul(masked, ident_b[:], mask_b[:].unsqueeze(1).to_broadcast([P, len(heads), P]),
                                 start=True, stop=False, skip_group_check=True)
                for j, h in enumerate(heads):
                    last = nc.tensor.matmul(bank[:, keys * j:keys * j + keys],
                                            q_rows[0:SPLIT_ROWS, b % 2, h, P * qt:P * qt + P],
                                            k_rows[0:SPLIT_ROWS, b % 2, h, 0:keys],
                                            start=False, stop=(j == len(heads) - 1), skip_group_check=True)
                last.then_inc(s_ready, 1)

            def transpose_shift(b):
                job = ("shift", b)
                pe.wait_ge(shift_ready, b + 1)
                misc_begin(pe, job)
                for qt in range(QT):
                    last = nc.tensor.matmul(misc(job)[0:3 * NH, P * qt:P * qt + P],
                                            shift[:, b % 2, qt].rearrange("p a h -> p (a h)"), ident_b[:],
                                            start=True, stop=True)
                misc_end(last, job)

            def scores_t(b, g, u):
                n = NS * b + 3 * g + u
                if g == 0 and u == 0:
                    pe.wait_ge(shift_in[b % 2], 48 * (b // 2 + 1))
                if n >= 2:
                    pe.wait_ge(t_free, n - 1)
                bank = t_ps[n % 2]
                k, q = k_rows[0:ROWS, b % 2], q_rows[0:ROWS, b % 2]
                if u < 2:
                    for j in range(2):
                        h = GH * g + 2 * u + j
                        last = nc.tensor.matmul(bank[:, S * j:S * j + S], k[:, h, 0:P], q[:, h, :],
                                                start=True, stop=True)
                else:
                    for j in range(GH):
                        h = GH * g + j
                        last = nc.tensor.matmul(bank[:, P * j:P * j + P], k[:, h, P:], q[:, h, P:],
                                                start=True, stop=True)
                last.then_inc(t_ready, 1)

            def outputs(b, g):
                n = NG * b + g
                pe.wait_ge(probs_masked, 3 * (n + 1))
                if g == 0:
                    misc_copied(pe, ("v", b))
                if n >= 1:
                    pe.wait_ge(o_free, n)
                for j in range(GH):
                    nc.tensor.matmul(o_ps[32 * j:32 * j + 32, 0:S], v_ones[:, b % 3, 0, GH * g + j, :],
                                     probs[:, g % 2, j // 2, S * (j % 2):S * (j % 2) + S],
                                     start=True, stop=False)
                for j in range(GH):
                    last = nc.tensor.matmul(o_ps[32 * j:32 * j + 32, P:S], v_ones[:, b % 3, 1, GH * g + j, :],
                                            probs[:, g % 2, 2, P * j:P * j + P],
                                            start=False, stop=True)
                last.then_inc(o_ready, 1)

            def attention_end(b):
                pe.wait_ge(o_free, NG * (b + 1))
                for qt in range(QT):
                    job = ("ot", b, qt)
                    misc_begin(pe, job)
                    for g in range(NG):
                        last = nc.tensor.transpose(misc(job)[:, P * g:P * g + P], o_t[:, g, P * qt:P * qt + P], ident[:])
                    misc_end(last, job)
                job = ("at", b)
                for qt in range(QT):
                    misc_copied(pe, ("ot", b, qt))
                misc_begin(pe, job)
                for c in range(HC):
                    for qt in range(QT):
                        o = S * c + P * qt
                        v = attn[:, qt].rearrange("p h d -> p (h d)")
                        last = nc.tensor.transpose(misc(job)[:, o:o + P], v[:, P * c:P * c + P], ident[:])
                misc_end(last, job)
                misc_copied(pe, job)
                if b == 0:
                    pe.wait_ge(wo_in, 16)
                job = ("wo", b)
                misc_begin(pe, job)
                for qt in range(QT):
                    for c in range(HC):
                        last = nc.tensor.matmul(misc(job)[:, H * qt:H * qt + H],
                                                attn_t[:, S * c + P * qt:S * c + P * qt + P],
                                                wo[:, c, :], start=(c == 0), stop=(c == HC - 1))
                misc_end(last, job)

            def ffn_in(b):
                pe.wait_ge(xn2_ready, b + 1)
                job = ("x2", b)
                misc_begin(pe, job)
                for c in range(HC):
                    for t in range(QT):
                        o = S * c + P * t
                        last = nc.tensor.transpose(misc(job)[:, o:o + P], xn2[:, b % 2, t, P * c:P * c + P], ident[:])
                misc_end(last, job)
                misc_copied(pe, job)
                if b == 0:
                    pe.wait_ge(gate_in, 16)
                job = ("logits", b)
                misc_begin(pe, job)
                for t in range(QT):
                    for c in range(HC):
                        o = S * b + P * t
                        last = nc.tensor.matmul(misc(job)[:, E * t:E * t + E], xn2_t[:, c, o:o + P], gate[:, c, :],
                                                start=(c == 0), stop=(c == HC - 1))
                misc_end(last, job)

            def shared(b):
                if b == 0:
                    pe.wait_ge(sw_in, 48)
                for c, (at, size) in enumerate(SC):
                    n = gu_no(b, c)
                    if n >= 2:
                        pe.wait_ge(mid_done, n - 1)
                    else:
                        pe.wait_ge(s_free, NS * B)
                    for half in range(2):
                        for hc in range(HC):
                            last = nc.tensor.matmul(s_ps[n % 2][0:size, S * half:S * half + S],
                                                    sgu[:, hc, half, at:at + size], xn2_t[:, hc, S * b:S * b + S],
                                                    start=(hc == 0), stop=(hc == HC - 1))
                    last.then_inc(gu_ready, 1)
                job = ("shared", b)
                misc_begin(pe, job)
                pe.wait_ge(mid_done, gu_no(b, SHARED - 1) + 1)
                for qt in range(QT):
                    for c, (_, size) in enumerate(SC):
                        last = nc.tensor.matmul(misc(job)[:, H * qt:H * qt + H],
                                                s_mid[0:size, c, P * qt:P * qt + P], sdn[0:size, c, :],
                                                start=(c == 0), stop=(c == SHARED - 1))
                misc_end(last, job)

            def ranks():
                job = ("rank",)
                pe.wait_ge(chosen_ready, 1)
                misc_begin(pe, job)
                v = misc(job)[:, 0:NT * E].rearrange("p (t e) -> p t e", t=NT)
                nc.tensor.matmul(v, above_b[:], chosen_b[:], start=True, stop=False, skip_group_check=True)
                for t in range(NT - 1):
                    later = NT - 1 - t
                    last = nc.tensor.matmul(v[:, t + 1:, :], ones_b[:],
                                            chosen_b[:, t, :].unsqueeze(1).to_broadcast([P, later, E]),
                                            start=False, stop=(later == 1), skip_group_check=True)
                misc_end(last, job)

            def slots(g):
                job = ("slots", g)
                misc_begin(pe, job)
                if g == 0:
                    pe.wait_ge(vals_ready, 1)
                for j in range(EG):
                    e = EG * g + j
                    pe.wait_ge(onehot_ready, e + 1)
                    for t in range(NT):
                        last = nc.tensor.matmul(misc(job)[:, 6 * j:6 * j + 6], onehot[:, j, t, :], tok_vals[:, t, e, :],
                                                start=(t == 0), stop=(t == NT - 1))
                    if j < EG - 1:
                        last.then_inc(onehot_used, 1)
                    else:
                        misc_end(last, job)
                n = MISC_NO[job]
                pe.wait_ge(misc_ready[n % MISC_BANKS], n // MISC_BANKS + 1)
                pe.sem_inc(onehot_used, 1)

            def expert_in(e):
                pe.wait_ge(gathered[e % 3], 16 * (e // 3 + 1))
                if e < 2:
                    pe.wait_ge(t_free, NS * B)
                else:
                    pe.wait_ge(xg_t_ready, e - 1)
                for c in range(HC):
                    last = nc.tensor.transpose(t_ps[e % 2][:, P * c:P * c + P], xg[:, e % 3, P * c:P * c + P], ident[:])
                last.then_inc(xgt_ready, 1)

            def expert_up(e):
                n = gu_of(e)
                if e % EG == 0:
                    pe.wait_ge(ew_in[(e // EG) % 2], 32 * (e // EG // 2 + 1))
                pe.wait_ge(xg_t_ready, e + 1)
                pe.wait_ge(mid_done, n - 1)
                w = wgu[:, (e // EG) % 2, e % EG]
                for half in range(2):
                    for c in range(2):
                        for hc in range(HC):
                            o = 2 * CAP * half + CAP * c
                            last = nc.tensor.matmul(s_ps[n % 2][0:IC, o:o + CAP], w[:, hc, half, IC * c:IC * c + IC],
                                                    xg_t[:, e % 2, hc, :], start=(hc == 0), stop=(hc == HC - 1))
                last.then_inc(gu_ready, 1)

            def expert_down(e):
                job = ("down", e)
                misc_begin(pe, job)
                pe.wait_ge(mid_done, gu_of(e) + 1)
                for c in range(2):
                    last = nc.tensor.matmul(misc(job)[:, 0:H], e_mid[:, e % 2, c, :],
                                            wdn[:, (e // EG) % 2, e % EG, c, :], start=(c == 0), stop=(c == 1))
                misc_end(last, job)

            keys_values(0)
            queries(0)
            keys_values(1)
            queries(1)
            for u in range(NS):
                scores(0, u)
            transpose_shift(0)
            keys_values(2)
            queries(2)
            for b in range(B):
                for g in range(NG):
                    for u in range(3):
                        scores_t(b, g, u)
                        if b + 1 < B:
                            scores(b + 1, 3 * g + u)
                    if g >= 1:
                        outputs(b, g - 1)
                    if g == 2 and b >= 1:
                        ffn_in(b - 1)
                outputs(b, NG - 1)
                if b + 1 < B:
                    transpose_shift(b + 1)
                attention_end(b)
                if b + 3 < B:
                    keys_values(b + 3)
                    queries(b + 3)
            shared(0)
            shared(1)
            ffn_in(B - 1)
            shared(2)
            shared(3)
            ranks()
            slots(0)
            expert_in(0)
            expert_up(0)
            for e in range(E):
                if e + 1 < E:
                    expert_in(e + 1)
                if e % EG == 1 and e // EG + 1 < E // EG:
                    slots(e // EG + 1)
                if e + 1 < E:
                    expert_up(e + 1)
                expert_down(e)


def kernel(x, ctx_512, L0_xattn_Wq, L0_xattn_Wkv_expand, L0_xattn_Wout, L0_ffn_gate_w, L0_ffn_w_gate,
           L0_ffn_w_up, L0_ffn_w_down, L0_ffn_sw_gate, L0_ffn_sw_up, L0_ffn_sw_down):
    import numpy as np
    import concourse.bacc as bacc
    from concourse.bass_utils import run_bass_kernel_spmd

    def lay(a, *axes):
        return np.ascontiguousarray(np.asarray(a).transpose(*axes))

    gate_up = np.stack([np.asarray(L0_ffn_w_gate), np.asarray(L0_ffn_w_up)]).reshape(2, E, HC, P, I)
    down = np.asarray(L0_ffn_w_down).reshape(E, 2, IC, H)
    arrays = {
        "in_x": np.ascontiguousarray(np.asarray(x)),
        "in_ctx_t": lay(ctx_512, 0, 2, 1),
        "in_wq_t": lay(L0_xattn_Wq, 1, 0),
        "in_wkv_t": lay(L0_xattn_Wkv_expand, 1, 0),
        "in_wo_t": lay(L0_xattn_Wout, 1, 0),
        "in_gate_t": lay(L0_ffn_gate_w, 1, 0),
        "in_w_gu": lay(gate_up, 3, 1, 2, 0, 4),
        "in_w_dn": lay(down, 2, 0, 1, 3),
        "in_sw_gu": lay(np.stack([np.asarray(L0_ffn_sw_gate), np.asarray(L0_ffn_sw_up)]), 1, 0, 2),
        "in_sw_dn": np.ascontiguousarray(np.asarray(L0_ffn_sw_down)),
    }
    nc = bacc.Bacc("TRN2", target_bir_lowering=False, num_devices=1)
    args = [nc.dram_tensor(n, a.shape, mybir.dt.from_np(a.dtype), kind="ExternalInput").ap()
            for n, a in arrays.items()]
    out = nc.dram_tensor("out_0", (B, S, H), F32, kind="ExternalOutput").ap()
    build(nc, *args, out)
    r = run_bass_kernel_spmd(nc, [arrays], core_ids=[0])
    return r.results[0]["out_0"]
```

```python
from contextlib import ExitStack

import concourse.bass as bass
from concourse import mybir
from concourse.alu_op_type import AluOpType as ALU

F32 = mybir.dt.float32
BF16 = mybir.dt.bfloat16
I32 = mybir.dt.int32
ACT = mybir.ActivationFunctionType
AX = mybir.AxisListType

P = 128
B, S, H = 4, 256, 256
NT = B * S // P
NH, HD = 16, 16
L = 64
HC = H // P
QT = S // P
GH = 4
NG = NH // GH
E, TOPK, I = 16, 4, 176
IC = 88
IS = 352
SC = ((0, 128), (128, 128), (256, 96))
CAP = 128
T = B * S
EG = 4
GATHERS = 6
EPS = 1e-5
FLOOR = -87.33
NEG = -(2.0 ** 127)

Q_PARTS = ((0, 3), (1, 2), (2, 1))
K_PARTS = ((0, 1, 2), (0, 1), (0,))
SPLIT_ROWS = 6 * HD
SHIFT_ROWS = 3
ROWS = SPLIT_ROWS + SHIFT_ROWS


SLOT_GROUPS = ((0, 1), (2, 3), (4, 5, 6, 7), (8, 9, 10, 11), (12, 13, 14, 15))
GROUP_OF = {e: g for g, experts in enumerate(SLOT_GROUPS) for e in experts}
EARLY_GROUPS = 3
SHARED_FILL = {
    1: ((("gu", 0, 0),), (("gu", 0, 1),), (("gu", 0, 2),)),
    2: ((("shared", 0),), (("gu", 1, 0),), (("gu", 1, 1),)),
    3: ((("gu", 1, 2),), (("shared", 1),), (("gu", 2, 0), ("gu", 2, 1))),
}


def pe_order():
    steps = []

    def proj(b):
        steps.extend([("k", b), ("v", b), ("x", b), ("q", b)])

    for b in range(3):
        proj(b)
    steps.extend(("s", 0, u) for u in range(3 * NG))
    steps.append(("shift", 0))
    proj(3)
    for b in range(B):
        for g in range(NG):
            for u in range(3):
                steps.append(("st", b, g, u))
                if b + 1 < B:
                    steps.append(("s", b + 1, 3 * g + u))
            if g >= 1:
                steps.append(("o", b, g - 1))
            if g == 1 and b >= 1:
                steps.extend([("x2", b - 1), ("logits", b - 1)])
        steps.append(("o", b, NG - 1))
        if b + 1 < B:
            steps.append(("shift", b + 1))
        fill = SHARED_FILL.get(b, ((), (), ()))
        steps.extend([("ot", b, 0), ("ot", b, 1), *fill[0], ("at", b), *fill[1], ("wo", b), *fill[2]])
    steps.extend([("x2", B - 1), ("logits", B - 1), ("gu", 2, 2), ("shared", 2), ("gu", 3, 0), ("rank",),
                  ("gu", 3, 1), ("gu", 3, 2), ("slots", 0), ("shared", 3), ("slots", 1), ("slots", 2), ("in", 0), ("in", 1)])
    for e in range(E + 2):
        if e < E:
            steps.append(("up", e))
        if 1 <= e <= E:
            steps.append(("turn", e - 1))
        if e + 2 < E:
            steps.append(("in", e + 2))
        if e in (4, 8):
            steps.append(("slots", EARLY_GROUPS + e // 4 - 1))
        if e >= 2:
            steps.append(("down", e - 2))
    return steps


PE_ORDER = pe_order()


class Ring:

    def __init__(self, ctx, nc, name, banks, kinds):
        self.banks = [ctx.enter_context(nc.psum_tensor(f"{name}_ps{i}", [P, 512], F32)) for i in range(banks)]
        self.ready = [ctx.enter_context(nc.semaphore(f"{name}_ready{i}")) for i in range(banks)]
        self.free = [ctx.enter_context(nc.semaphore(f"{name}_free{i}")) for i in range(banks)]
        self.at = {}
        for job in PE_ORDER:
            if job[0] in kinds:
                n = len(self.at)
                self.at[job] = n % banks, n // banks

    def bank(self, job):
        return self.banks[self.at[job][0]]

    def begin(self, pe, job):
        i, turn = self.at[job]
        if turn:
            pe.wait_ge(self.free[i], turn)

    def filled(self, ins, job):
        ins.then_inc(self.ready[self.at[job][0]], 1)

    def wait(self, eng, job):
        i, turn = self.at[job]
        eng.wait_ge(self.ready[i], turn + 1)

    def emptied(self, ins, job):
        ins.then_inc(self.free[self.at[job][0]], 1)

    def wait_emptied(self, eng, job):
        i, turn = self.at[job]
        eng.wait_ge(self.free[i], turn + 1)


def build(nc, x, ctx_t, wq_t, wkv_t, wo_t, gate_t, w_gu, w_dn, sw_gu, sw_dn, out):
    q_parts_d = nc.dram_tensor("q_parts_d", [B, 3, H, S], BF16, kind="Internal").ap()
    k_parts_d = nc.dram_tensor("k_parts_d", [B, 3, H, S], BF16, kind="Internal").ap()
    xn2_d = nc.dram_tensor("xn2_d", [T + CAP, H], F32, kind="Internal").ap()

    with ExitStack() as ctx:
        def sb(name, shape, dt=F32):
            return ctx.enter_context(nc.sbuf_tensor(name, shape, dt))

        def sem(name):
            return ctx.enter_context(nc.semaphore(name))

        ident = sb("ident", [P, P])
        ident_b = sb("ident_b", [P, P], BF16)
        above_b = sb("above_b", [P, P], BF16)
        ones_b = sb("ones_b", [P, P], BF16)
        mask_b = sb("mask_b", [P, P], BF16)
        slot_iota = sb("slot_iota", [P, P], BF16)
        cst = sb("cst", [P, P])
        spare_row = sb("spare_row", [P, 1])
        eps = sb("eps", [P, 1])
        zero_rows = sb("zero_rows", [P, H])
        wq = sb("wq", [P, HC, H])
        wkv = sb("wkv", [L, 2 * H])
        wo = sb("wo", [P, HC, H])
        gate = sb("gate", [P, HC, E])
        sgu = sb("sgu", [P, HC, 2, IS])
        sdn = sb("sdn", [P, 3, H])
        wgu = sb("wgu", [P, 2, EG, HC, 2, I])
        wdn = sb("wdn", [IC, 2, EG, 2, H])
        lat = sb("lat", [L, B, S])
        xs = sb("xs", [P, NT, H])
        xn = sb("xn", [P, 2, QT, H])
        xn_t = sb("xn_t", [P, HC * S])
        stats = sb("stats", [P, NT, 6])
        mv = sb("mv", [P, NT, 2])
        std = sb("std", [P, NT])
        rstd = sb("rstd", [P, NT])
        parts = {k: sb(f"{k}_parts", [P, 2, 3, 2 * S], BF16) for k in "kq"}
        rest = sb("rest", [P, 2, 2 * S])
        q_rows = sb("q_rows", [P, 2, NH, S], BF16)
        k_rows = sb("k_rows", [P, 2, NH, S], BF16)
        v_ones = sb("v_ones", [P, B, QT, NH, 2 * HD])
        top = sb("top", [P, 2, QT, NH])
        shift = sb("shift", [P, 2, QT, 3, NH], BF16)
        shift_rest = sb("shift_rest", [P, QT, NH])
        shift_t = sb("shift_t", [3 * NH, 2, S], BF16)
        probs = sb("probs", [P, 2, 3, 2 * S])
        o_t = sb("o_t", [P, NG, S])
        den = sb("den", [P, QT, NH])
        attn = sb("attn", [P, QT, NH, HD])
        attn_t = sb("attn_t", [P, HC * S])
        stats2 = sb("stats2", [P, NT, 6])
        mv2 = sb("mv2", [P, NT, 2])
        std2 = sb("std2", [P, NT])
        rstd2 = sb("rstd2", [P, NT])
        xn2 = sb("xn2", [P, 2, QT, H])
        xn2_t = sb("xn2_t", [P, HC, T])
        logits = sb("logits", [P, NT, E])
        score = sb("score", [P, NT, E])
        r1 = sb("r1", [P, NT])
        r2 = sb("r2", [P, NT])
        best = sb("best", [P, NT, 8])
        above4 = sb("above4", [P, NT, E])
        tied = sb("tied", [P, NT, E])
        PAD = 8
        run_a = sb("run_a", [P, NT, PAD + E])
        run_b = sb("run_b", [P, NT, PAD + E])
        chosen = sb("chosen", [P, NT, E])
        chosen_b = sb("chosen_b", [P, NT, E], BF16)
        weight = sb("weight", [P, NT, E])
        kept = sb("kept", [P, NT, E])
        slot = sb("slot", [P, NT, E])
        tok_vals = sb("tok_vals", [P, NT, E, 6], BF16)
        onehot = sb("onehot", [P, EG, NT, CAP], BF16)
        slot_vals = sb("slot_vals", [P, EG, 6])
        tok_f = sb("tok_f", [P, EG])
        empty = sb("empty", [P, EG])
        tok_i = sb("tok_i", [P, E], I32)
        slot_w = sb("slot_w", [P, E])
        s_act = sb("s_act", [P, 2, S])
        s_mid = sb("s_mid", [P, 3, S])
        xg = [xn[:, i // QT, i % QT, :] for i in range(2 * QT)]
        xg += [attn_t[:, H * i:H * i + H] for i in range(GATHERS - 2 * QT)]
        xg_t = sb("xg_t", [P, 2, HC, CAP])
        e_act = sb("e_act", [P, 2, I])
        e_mid = sb("e_mid", [P, 2, I])
        e_mid_t = sb("e_mid_t", [IC, 2, 2, CAP])
        y_rows = sb("y_rows", [P, 3, H])

        s_ring = Ring(ctx, nc, "s", 2, ("s", "gu", "up"))
        t_ring = Ring(ctx, nc, "t", 2, ("st", "in"))
        o_ring = Ring(ctx, nc, "o", 1, ("o", "turn"))
        m_ring = Ring(ctx, nc, "m", 3, ("k", "v", "x", "q", "shift", "ot", "at", "wo", "x2", "logits",
                                        "shared", "rank", "slots", "down"))

        consts = sem("consts")
        pool_chain = sem("pool_chain")
        dve_chain = sem("dve_chain")
        x_in = [sem(f"x_in{b}") for b in range(B)]
        lat_in = sem("lat_in")
        wkv_in = sem("wkv_in")
        wq_in = sem("wq_in")
        wo_in = sem("wo_in")
        gate_in = sem("gate_in")
        sw_in = sem("sw_in")
        ew_in = [sem(f"ew_in{i}") for i in range(2)]
        var_ready = sem("var_ready")
        std_ready = sem("std_ready")
        xn_ready = sem("xn_ready")
        lead_ready = sem("lead_ready")
        rest_ready = sem("rest_ready")
        mid_ready = sem("mid_ready")
        low_ready = sem("low_ready")
        stored = {k: [sem(f"{k}_stored{b}") for b in range(B)] for k in "kq"}
        rows_in = {k: [sem(f"{k}_rows_in{i}") for i in range(2)] for k in "kq"}
        shift_in = [sem(f"shift_in{i}") for i in range(2)]
        shift_ready = sem("shift_ready")
        probs_masked = sem("probs_masked")
        var2_ready = sem("var2_ready")
        std2_ready = sem("std2_ready")
        xn2_ready = sem("xn2_ready")
        xn2_stored = [sem(f"xn2_stored{i}") for i in range(2)]
        zeros_stored = sem("zeros_stored")
        z_ready = sem("z_ready")
        exp_ready = sem("exp_ready")
        chosen_ready = sem("chosen_ready")
        vals_ready = sem("vals_ready")
        onehot_ready = sem("onehot_ready")
        tok_ready = sem("tok_ready")
        act_ready = sem("act_ready")
        acc_stored = sem("acc_stored")
        gathered = [sem(f"gathered{i}") for i in range(GATHERS)]
        scattered = sem("scattered")

        NS = 3 * NG
        GU = {job: n for n, job in enumerate(j for j in PE_ORDER if j[0] in ("gu", "up"))}
        GU_JOBS = list(GU)

        block = ctx.enter_context(nc.Block())

        @block.sync
        def _(sp):
            sp.dma_start(xs[:, 0:QT, :], x[0].rearrange("(t p) c -> p t c", p=P)).then_inc(x_in[0], 16)
            sp.dma_start(lat[:, 0, :], ctx_t[0, :, 0:S]).then_inc(lat_in, 16)
            sp.dma_start(wkv[:], wkv_t).then_inc(wkv_in, 16)
            sp.dma_start(wq[:], wq_t.rearrange("(c p) n -> p c n", p=P)).then_inc(wq_in, 16)
            sp.dma_start(xs[:, QT:2 * QT, :], x[1].rearrange("(t p) c -> p t c", p=P)).then_inc(x_in[1], 16)
            sp.dma_start(lat[:, 1:B, :], ctx_t[1:B, :, 0:S].rearrange("b l k -> l b k")).then_inc(lat_in, 16)
            for b in range(2, B):
                sp.dma_start(xs[:, QT * b:QT * b + QT, :],
                             x[b].rearrange("(t p) c -> p t c", p=P)).then_inc(x_in[b], 16)

            def store_parts(b):
                for n, (k, d) in enumerate((("k", k_parts_d), ("q", q_parts_d))):
                    sp.wait_ge(low_ready, 2 * b + n + 1)
                    sp.dma_start(d[b].rearrange("a (m p) t -> p (a m) t", p=P),
                                 parts[k][:, b % 2].rearrange("p a (m t) -> p (a m) t", m=2)
                                 ).then_inc(stored[k][b], 16)

            def load_rows(b):
                if b >= 2:
                    t_ring.wait(sp, ("st", b - 2, NG - 1, 2))
                sp.wait_ge(stored["k"][b], 16)
                src = k_parts_d[b].rearrange("a (h d) t -> a d h t", d=HD)
                row = 0
                for group in K_PARTS:
                    for part in group:
                        sp.dma_start(k_rows[row:row + HD, b % 2], src[part]).then_inc(rows_in["k"][b % 2], 16)
                        row += HD
                sp.wait_ge(stored["q"][b], 16)
                src = q_parts_d[b].rearrange("a (h d) t -> a d h t", d=HD)
                row = 0
                for part, copies in Q_PARTS:
                    for _ in range(copies):
                        sp.dma_start(q_rows[row:row + HD, b % 2], src[part]).then_inc(rows_in["q"][b % 2], 16)
                        row += HD

            store_parts(0)
            load_rows(0)
            store_parts(1)
            load_rows(1)
            sp.dma_start(wo[:], wo_t.rearrange("(c p) n -> p c n", p=P)).then_inc(wo_in, 16)
            sp.dma_start(gate[:], gate_t.rearrange("(c p) n -> p c n", p=P)).then_inc(gate_in, 16)
            sp.dma_start(sgu[:], sw_gu.rearrange("(c p) g i -> p c g i", p=P)).then_inc(sw_in, 16)
            sp.dma_start(sdn[:, 0:2, :], sw_dn[0:2 * P].rearrange("(c p) n -> p c n", p=P)).then_inc(sw_in, 16)
            sp.dma_start(sdn[0:IS - 2 * P, 2, :], sw_dn[2 * P:IS]).then_inc(sw_in, 16)

            def store_base(b):
                m_ring.wait_emptied(sp, ("shared", b))
                sp.dma_start(out[S * b:S * b + S].rearrange("(t p) c -> p t c", p=P),
                             xs[:, QT * b:QT * b + QT]).then_inc(acc_stored, 16)

            def load_experts(g):
                if g >= 2:
                    m_ring.wait(sp, ("down", EG * (g - 1) - 1))
                sp.dma_start(wgu[:, g % 2], w_gu[:, EG * g:EG * g + EG]).then_inc(ew_in[g % 2], 16)
                sp.dma_start(wdn[:, g % 2], w_dn[:, EG * g:EG * g + EG]).then_inc(ew_in[g % 2], 16)

            store_parts(2)
            store_parts(3)
            load_experts(0)
            load_experts(1)
            for b in range(B):
                if b + 2 < B:
                    load_rows(b + 2)
                sp.wait_ge(xn2_ready, b + 1)
                sp.dma_start(xn2_d[S * b:S * b + S].rearrange("(t p) c -> p t c", p=P),
                             xn2[:, b % 2]).then_inc(xn2_stored[b % 2], 16)
                if b >= 2:
                    store_base(b - 2)
            store_base(2)
            store_base(3)
            load_experts(2)
            load_experts(3)
            sp.wait_ge(scattered, 16 * E)

        @block.gpsimd
        def _(pool):
            n_chain = [0]

            def link(ins):
                n_chain[0] += 1
                ins.then_inc(pool_chain, 1)
                pool.wait_ge(pool_chain, n_chain[0])

            n_const = [0]

            def constant(ins):
                n_const[0] += 1
                ins.then_inc(consts, 1)
                pool.wait_ge(consts, n_const[0])

            constant(nc.gpsimd.memset(eps[:], EPS))
            link(nc.gpsimd.memset(ident[:], 0.0))
            constant(nc.gpsimd.affine_select(out=ident[:], in_=ident[:], compare_op=ALU.not_equal, fill=1.0,
                                             base=0, pattern=[[-1, P]], channel_multiplier=1))
            constant(nc.gpsimd.tensor_copy(ident_b[:], ident[:]))
            link(nc.gpsimd.memset(cst[:], 0.0))
            link(nc.gpsimd.affine_select(out=cst[:], in_=cst[:], compare_op=ALU.is_ge, fill=NEG,
                                         base=0, pattern=[[-1, P]], channel_multiplier=1))
            constant(nc.gpsimd.tensor_copy(mask_b[:], cst[:]))
            link(nc.gpsimd.memset(v_ones[:, :, :, :, HD:], 1.0))
            constant(nc.gpsimd.memset(k_rows[SPLIT_ROWS:P].rearrange("r b h t -> r (b h t)").bitcast(F32),
                                      1.0 + 0x3F80 / 2 ** 23))
            constant(nc.gpsimd.memset(zero_rows[:], 0.0))
            pool.dma_start(xn2_d[T:T + CAP], zero_rows[:]).then_inc(zeros_stored, 16)
            pool.dma_start(out[T:T + CAP], zero_rows[:]).then_inc(zeros_stored, 16)

            def last_parts(b):
                for n, k in enumerate("kq"):
                    pool.wait_ge(mid_ready, 2 * b + n + 1)
                    if b >= 2:
                        pool.wait_ge(stored[k][b - 2], 16)
                    nc.gpsimd.tensor_tensor(parts[k][:, b % 2, 2, :], rest[:, n, :], parts[k][:, b % 2, 1, :],
                                            ALU.subtract).then_inc(low_ready, 1)

            def causal(b, g):
                for u in range(3):
                    t_ring.wait_emptied(pool, ("st", b, g, u))
                    if u < 2:
                        v = probs[:, g % 2, u, :].rearrange("p (h q) -> p h q", h=2)[:, :, 0:P]
                    else:
                        v = probs[:, g % 2, u, :].rearrange("p (h q) -> p h q", h=GH)
                    nc.gpsimd.affine_select(out=v, in_=v, compare_op=ALU.is_ge, fill=0.0, base=0,
                                            pattern=[[0, v.shape[1]], [1, P]],
                                            channel_multiplier=-1).then_inc(probs_masked, 1)

            last_parts(0)
            last_parts(1)
            last_parts(2)
            link(nc.gpsimd.memset(cst[:], 1.0))
            link(nc.gpsimd.tensor_copy(ones_b[:], cst[:]))
            link(nc.gpsimd.affine_select(out=cst[:], in_=cst[:], compare_op=ALU.is_gt, fill=0.0,
                                         base=0, pattern=[[1, P]], channel_multiplier=-1))
            link(nc.gpsimd.tensor_copy(above_b[:], cst[:]))
            link(nc.gpsimd.iota(cst[:], pattern=[[1, P]], base=1, channel_multiplier=0,
                                allow_small_or_imprecise_dtypes=True))
            link(nc.gpsimd.tensor_copy(slot_iota[:], cst[:]))
            link(nc.gpsimd.iota(spare_row[:], pattern=[[0, 1]], base=T, channel_multiplier=1,
                                allow_small_or_imprecise_dtypes=True))
            link(nc.gpsimd.iota(cst[:], pattern=[[0, P]], base=0, channel_multiplier=1,
                                allow_small_or_imprecise_dtypes=True))
            v = cst[:].rearrange("p (t e) -> p t e", t=NT)
            link(nc.gpsimd.tensor_copy(tok_vals[:, :, :, 0], v))
            link(nc.gpsimd.iota(v, pattern=[[P, NT], [0, E]], base=0, channel_multiplier=0,
                                allow_small_or_imprecise_dtypes=True))
            link(nc.gpsimd.tensor_copy(tok_vals[:, :, :, 1], v))
            link(nc.gpsimd.memset(cst[:], 1.0))
            link(nc.gpsimd.tensor_copy(tok_vals[:, :, :, 2], v))
            link(nc.gpsimd.memset(run_a[:], 0.0))
            constant(nc.gpsimd.memset(run_b[:], 0.0))
            last_parts(3)
            for b in range(B):
                for g in range(NG):
                    causal(b, g)

            def gather(e):
                if e == 0:
                    pool.wait_ge(xn2_stored[0], 32)
                    pool.wait_ge(xn2_stored[1], 32)
                    pool.wait_ge(zeros_stored, 32)
                pool.wait_ge(tok_ready, GROUP_OF[e] + 1)
                if e >= GATHERS:
                    t_ring.wait(pool, ("in", e - GATHERS))
                nc.gpsimd.indirect_dma_start(
                    out=xg[e % GATHERS], out_offset=None, in_=xn2_d[:, :],
                    in_offset=bass.IndirectOffsetOnAxis(ap=tok_i[:, e:e + 1], axis=0),
                ).then_inc(gathered[e % GATHERS], 16)

            def scatter(e):
                m_ring.wait_emptied(pool, ("down", e))
                if e == 0:
                    pool.wait_ge(acc_stored, 16 * B)
                else:
                    pool.wait_ge(scattered, 16 * e)
                nc.gpsimd.indirect_dma_start(
                    out=out[:, :], out_offset=bass.IndirectOffsetOnAxis(ap=tok_i[:, e:e + 1], axis=0),
                    in_=y_rows[:, e % 3, :], in_offset=None, compute_op=ALU.add,
                ).then_inc(scattered, 16)

            for e in range(GATHERS):
                gather(e)
            for e in range(E):
                if e + GATHERS < E:
                    gather(e + GATHERS)
                scatter(e)

        @block.scalar
        def _(act):
            def sqrt_var(lo, hi, src, dst, done):
                nc.scalar.activation(dst[:, lo:hi], src[:, lo:hi, 1], ACT.Sqrt, bias=eps[:, 0:1]).then_inc(done, 1)

            def copy_k(b):
                m_ring.wait(act, ("k", b))
                if b >= 2:
                    act.wait_ge(stored["k"][b - 2], 16)
                nc.scalar.activation(parts["k"][:, b % 2, 0, :], m_ring.bank(("k", b))[:], ACT.Copy).then_inc(lead_ready, 1)

            def copy_rest(b):
                m_ring.wait(act, ("v", b))
                m_ring.emptied(nc.scalar.activation(
                    v_ones[:, b, :, :, 0:HD],
                    m_ring.bank(("v", b))[:].rearrange("p (c h d) -> p c h d", c=QT, h=NH), ACT.Copy), ("v", b))
                m_ring.wait(act, ("x", b))
                if b >= 1:
                    m_ring.wait(act, ("q", b - 1))
                misc_x = nc.scalar.activation(xn_t[:], m_ring.bank(("x", b))[:], ACT.Copy)
                m_ring.emptied(misc_x, ("x", b))
                m_ring.wait(act, ("q", b))
                if b >= 2:
                    act.wait_ge(stored["q"][b - 2], 16)
                nc.scalar.activation(parts["q"][:, b % 2, 0, :], m_ring.bank(("q", b))[:], ACT.Copy).then_inc(lead_ready, 1)

            def exps(b, g, u):
                job = ("st", b, g, u)
                t_ring.wait(act, job)
                if NG * b + g >= 2:
                    o_ring.wait(act, ("o", b, g - 2) if g >= 2 else ("o", b - 1, g + 2))
                t_ring.emptied(nc.scalar.activation(probs[:, g % 2, u, :], t_ring.bank(job)[:], ACT.Exp,
                                                    scale=HD ** -0.5), job)

            def copy_o(b, g):
                o_ring.wait(act, ("o", b, g))
                if b >= 1 and g == 0:
                    m_ring.wait(act, ("ot", b - 1, 1))
                o_ring.emptied(nc.scalar.activation(o_t[:, g, :], o_ring.bank(("o", b, g))[:, 0:S], ACT.Copy),
                               ("o", b, g))

            def send_shift(b):
                m_ring.wait(act, ("shift", b))
                if b >= 2:
                    act.wait_ge(shift_in[b % 2], 48 * (b // 2))
                m_ring.emptied(nc.scalar.activation(shift_t[:, b % 2, :], m_ring.bank(("shift", b))[0:3 * NH, 0:S], ACT.Copy),
                          ("shift", b))
                m_ring.wait_emptied(act, ("shift", b))
                if b >= 2:
                    t_ring.wait(act, ("st", b - 2, NG - 1, 2))
                for r in range(3):
                    act.dma_start(q_rows[SPLIT_ROWS + r:SPLIT_ROWS + r + 1, b % 2],
                                  shift_t[NH * r:NH * r + NH, b % 2, :]).then_inc(shift_in[b % 2], 16)

            def copy_at(b):
                m_ring.wait(act, ("at", b))
                if b >= 1:
                    m_ring.wait(act, ("wo", b - 1))
                m_ring.emptied(nc.scalar.activation(attn_t[:], m_ring.bank(("at", b))[:], ACT.Copy), ("at", b))

            def copy_x2(b):
                m_ring.wait(act, ("x2", b))
                m_ring.emptied(nc.scalar.activation(
                    xn2_t[:, :, S * b:S * b + S],
                    m_ring.bank(("x2", b))[:].rearrange("p (c t) -> p c t", c=HC), ACT.Copy), ("x2", b))

            def std2_of(b):
                act.wait_ge(var2_ready, b + 1)
                sqrt_var(QT * b, QT * b + QT, mv2, std2, std2_ready)

            def silu(job, rows, cols, dst):
                n = GU[job]
                s_ring.wait(act, job)
                if n >= 2:
                    s_ring.wait_emptied(act, GU_JOBS[n - 2])
                nc.scalar.activation(dst[0:rows, n % 2, :], s_ring.bank(job)[0:rows, 0:cols],
                                     ACT.Silu).then_inc(act_ready, 1)

            def gu_silu(b, c):
                silu(("gu", b, c), SC[c][1], S, s_act)

            def copy_in(e):
                job = ("in", e)
                t_ring.wait(act, job)
                if e >= 2:
                    s_ring.wait(act, ("up", e - 2))
                t_ring.emptied(nc.scalar.activation(xg_t[:, e % 2].rearrange("p c s -> p (c s)"),
                                                    t_ring.bank(job)[:, 0:HC * CAP], ACT.Copy), job)

            def copy_turn(e):
                job = ("turn", e)
                o_ring.wait(act, job)
                if e >= 2:
                    m_ring.wait(act, ("down", e - 2))
                o_ring.emptied(nc.scalar.activation(e_mid_t[:, e % 2].rearrange("p c s -> p (c s)"),
                                                    o_ring.bank(job)[0:IC, 0:2 * CAP], ACT.Copy), job)

            act.wait_ge(consts, 1)
            act.wait_ge(var_ready, 1)
            sqrt_var(0, QT, mv, std, std_ready)
            copy_k(0)
            act.wait_ge(var_ready, B)
            sqrt_var(QT, NT, mv, std, std_ready)
            copy_rest(0)
            for b in (1, 2):
                copy_k(b)
                copy_rest(b)
            send_shift(0)
            copy_k(3)
            copy_rest(3)
            for b in range(B):
                for g in range(NG):
                    for u in range(3):
                        exps(b, g, u)
                    if g >= 1:
                        copy_o(b, g - 1)
                    if g == 0 and b >= 1:
                        std2_of(b - 1)
                    if g == 1 and b >= 1:
                        copy_x2(b - 1)
                copy_o(b, NG - 1)
                if b + 1 < B:
                    send_shift(b + 1)
                fill = SHARED_FILL.get(b, ((), (), ()))
                for stage in range(3):
                    if stage == 2 and b == B - 1:
                        std2_of(b)
                    for job in fill[stage]:
                        if job[0] == "gu":
                            gu_silu(*job[1:])
                    if stage == 0:
                        copy_at(b)
            copy_x2(B - 1)
            gu_silu(2, 2)
            act.wait_ge(z_ready, 1)
            nc.scalar.activation(score[:], logits[:], ACT.Exp).then_inc(exp_ready, 1)
            for c in range(len(SC)):
                gu_silu(3, c)
            copy_in(0)
            copy_in(1)
            for e in range(E + 1):
                if e < E:
                    silu(("up", e), P, I, e_act)
                if e >= 1:
                    copy_turn(e - 1)
                if e + 2 < E:
                    copy_in(e + 2)

        @block.vector
        def _(dve):
            n_chain = [0]

            def link(ins):
                n_chain[0] += 1
                ins.then_inc(dve_chain, 1)
                dve.wait_ge(dve_chain, n_chain[0])

            def wide(v, n):
                return v.unsqueeze(2).to_broadcast([P, v.shape[1], n])

            def norm_stats(src, b, st, m, done):
                for t in range(QT * b, QT * b + QT):
                    ins = nc.vector.bn_stats(out=st[:, t, :], in_=src[:, t, :])
                    if t % QT < QT - 1:
                        n_chain[0] += 1
                        ins.then_inc(dve_chain, 1)
                    else:
                        link(ins)
                for t in range(QT * b, QT * b + QT):
                    ins = nc.vector.bn_aggr(out=m[:, t, :], in_=st[:, t, :])
                    if t % QT < QT - 1:
                        link(ins)
                ins.then_inc(done, 1)

            def normalise(b):
                if b == 0:
                    dve.wait_ge(std_ready, 1)
                    link(nc.vector.reciprocal(rstd[:, 0:QT], std[:, 0:QT]))
                if b == 1:
                    dve.wait_ge(std_ready, 2)
                    link(nc.vector.reciprocal(rstd[:, QT:NT], std[:, QT:NT]))
                if b >= 2:
                    m_ring.wait(dve, ("x", b - 2))
                for t in range(QT):
                    k = QT * b + t
                    ins = nc.vector.tensor_scalar(xn[:, b % 2, t, :], xs[:, k, :], mv[:, k, 0:1], rstd[:, k:k + 1],
                                                  ALU.subtract, ALU.mult)
                    ins.then_inc(xn_ready, 1)

            def split(b, n, k):
                job = (k, b)
                dve.wait_ge(lead_ready, 2 * b + n + 1)
                if b >= 1:
                    dve.wait_ge(low_ready, 2 * (b - 1) + n + 1)
                m_ring.emptied(nc.vector.tensor_tensor(rest[:, n, :], m_ring.bank(job)[:], parts[k][:, b % 2, 0, :],
                                                  ALU.subtract), job)
                m_ring.wait_emptied(dve, job)
                nc.vector.tensor_copy(parts[k][:, b % 2, 1, :], rest[:, n, :]).then_inc(mid_ready, 1)

            def maxima(b, u):
                job = ("s", b, u)
                s_ring.wait(dve, job)
                if u < 4:
                    src = s_ring.bank(job)[:].rearrange("p (h k) -> p h k", h=GH)
                    dst = top[:, b % 2, 0, GH * u:GH * u + GH]
                else:
                    src = s_ring.bank(job)[:].rearrange("p (h k) -> p h k", h=2)
                    dst = top[:, b % 2, 1, 2 * (u - 4):2 * (u - 4) + 2]
                s_ring.emptied(nc.vector.tensor_reduce(dst, src, AX.X, ALU.max), job)

            def shift_parts(b):
                for u in (NS - 2, NS - 1):
                    s_ring.wait_emptied(dve, ("s", b, u))
                m, sh = top[:, b % 2], shift[:, b % 2]
                if b >= 2:
                    m_ring.wait(dve, ("shift", b - 2))
                link(nc.vector.tensor_scalar(sh[:, :, 0, :], m, -1.0, None, ALU.mult))
                link(nc.vector.scalar_tensor_tensor(out=shift_rest[:], in0=m, scalar=-1.0, in1=sh[:, :, 0, :],
                                                    op0=ALU.mult, op1=ALU.subtract))
                link(nc.vector.tensor_copy(sh[:, :, 1, :], shift_rest[:]))
                nc.vector.tensor_tensor(sh[:, :, 2, :], shift_rest[:], sh[:, :, 1, :],
                                        ALU.subtract).then_inc(shift_ready, 1)

            def attention_out(b, qt):
                job = ("ot", b, qt)
                m_ring.wait(dve, job)
                v = m_ring.bank(job)[:].rearrange("p (h r) -> p h r", h=NH)
                link(nc.vector.reciprocal(den[:, qt, :], v[:, :, HD]))
                if b >= 1:
                    m_ring.wait(dve, ("at", b - 1))
                m_ring.emptied(nc.vector.tensor_tensor(attn[:, qt], v[:, :, 0:HD], wide(den[:, qt, :], HD), ALU.mult), job)

            def add_residual(b):
                job = ("wo", b)
                m_ring.wait(dve, job)
                v = xs[:, QT * b:QT * b + QT, :]
                m_ring.emptied(nc.vector.tensor_tensor(v, m_ring.bank(job)[:].rearrange("p (t c) -> p t c", t=QT), v, ALU.add), job)
                m_ring.wait_emptied(dve, job)
                norm_stats(xs, b, stats2, mv2, var2_ready)

            def normalise2(b):
                dve.wait_ge(std2_ready, b + 1)
                link(nc.vector.reciprocal(rstd2[:, QT * b:QT * b + QT], std2[:, QT * b:QT * b + QT]))
                if b >= 2:
                    dve.wait_ge(xn2_stored[b % 2], 16 * (b // 2))
                    m_ring.wait(dve, ("x2", b - 2))
                for t in range(QT):
                    k = QT * b + t
                    ins = nc.vector.tensor_scalar(xn2[:, b % 2, t, :], xs[:, k, :], mv2[:, k, 0:1],
                                                  rstd2[:, k:k + 1], ALU.subtract, ALU.mult)
                    if t < QT - 1:
                        link(ins)
                ins.then_inc(xn2_ready, 1)

            def copy_logits(b):
                job = ("logits", b)
                m_ring.wait(dve, job)
                m_ring.emptied(nc.vector.tensor_copy(logits[:, QT * b:QT * b + QT, :],
                                                m_ring.bank(job)[:, 0:QT * E].rearrange("p (t e) -> p t e", t=QT)), job)

            def gu_mid(b, c):
                job, size = ("gu", b, c), SC[c][1]
                n = GU[job]
                dve.wait_ge(act_ready, n + 1)
                if b >= 1 and c == 0:
                    m_ring.wait(dve, ("shared", b - 1))
                s_ring.emptied(nc.vector.tensor_tensor(s_mid[0:size, c, :], s_ring.bank(job)[0:size, S:2 * S],
                                                       s_act[0:size, n % 2, :], ALU.mult), job)

            def shared_out(b):
                job = ("shared", b)
                m_ring.wait(dve, job)
                v = xs[:, QT * b:QT * b + QT, :]
                m_ring.emptied(nc.vector.tensor_tensor(v, m_ring.bank(job)[:].rearrange("p (t c) -> p t c", t=QT), v, ALU.add),
                               job)

            def route_start():
                for b in range(B):
                    m_ring.wait_emptied(dve, ("logits", b))
                link(nc.vector.tensor_reduce(r1[:], logits[:], AX.X, ALU.max))
                nc.vector.tensor_tensor(logits[:], logits[:], wide(r1[:], E), ALU.subtract).then_inc(z_ready, 1)
                dve.wait_ge(z_ready, 1)
                link(nc.vector.tensor_scalar(above4[:], logits[:], FLOOR, None, ALU.max))
                for t in range(NT):
                    ins = nc.vector.max(out=best[:, t, :], in_=above4[:, t, :])
                    n_chain[0] += 1
                    ins.then_inc(dve_chain, 1)
                dve.wait_ge(dve_chain, n_chain[0])
                dve.wait_ge(consts, 7)
                fourth = wide(best[:, :, TOPK - 1], E)
                link(nc.vector.tensor_tensor(run_a[:, :, PAD:], above4[:], fourth, ALU.is_equal))
                link(nc.vector.tensor_copy(tied[:], run_a[:, :, PAD:]))
                link(nc.vector.tensor_tensor(above4[:], above4[:], fourth, ALU.is_gt))
                link(nc.vector.tensor_reduce(r1[:], above4[:], AX.X, ALU.add))
                src, dst = run_a, run_b
                for step in (1, 2, 4, 8):
                    link(nc.vector.tensor_tensor(dst[:, :, PAD:], src[:, :, PAD:],
                                                 src[:, :, PAD - step:PAD + E - step], ALU.add))
                    src, dst = dst, src
                link(nc.vector.tensor_tensor(chosen[:], src[:, :, PAD:], wide(r1[:], E), ALU.add))
                link(nc.vector.scalar_tensor_tensor(out=chosen[:], in0=chosen[:], scalar=float(TOPK), in1=tied[:],
                                                    op0=ALU.is_le, op1=ALU.mult))
                link(nc.vector.tensor_tensor(chosen[:], chosen[:], above4[:], ALU.add))
                nc.vector.tensor_copy(chosen_b[:], chosen[:]).then_inc(chosen_ready, 1)

            def route_weights():
                dve.wait_ge(exp_ready, 1)
                link(nc.vector.tensor_reduce(r1[:], score[:], AX.X, ALU.add))
                link(nc.vector.reciprocal(r2[:], r1[:]))
                link(nc.vector.tensor_tensor(score[:], score[:], wide(r2[:], E), ALU.mult))
                link(nc.vector.tensor_tensor(score[:], score[:], chosen[:], ALU.mult))
                link(nc.vector.tensor_reduce(r1[:], score[:], AX.X, ALU.add))
                link(nc.vector.tensor_scalar(r1[:], r1[:], 1e-20, None, ALU.add))
                link(nc.vector.reciprocal(r2[:], r1[:]))
                link(nc.vector.tensor_tensor(weight[:], score[:], wide(r2[:], E), ALU.mult))
                link(nc.vector.tensor_copy(tok_vals[:, :, :, 3], weight[:]))
                link(nc.vector.tensor_tensor(weight[:], weight[:], tok_vals[:, :, :, 3], ALU.subtract))
                link(nc.vector.tensor_copy(tok_vals[:, :, :, 4], weight[:]))
                nc.vector.tensor_tensor(tok_vals[:, :, :, 5], weight[:], tok_vals[:, :, :, 4],
                                        ALU.subtract).then_inc(vals_ready, 1)

            def slots_of_tokens():
                job = ("rank",)
                m_ring.wait(dve, job)
                rank = m_ring.bank(job)[:, 0:NT * E].rearrange("p (t e) -> p t e", t=NT)
                link(nc.vector.scalar_tensor_tensor(out=kept[:], in0=rank, scalar=float(CAP), in1=chosen[:],
                                                    op0=ALU.is_lt, op1=ALU.mult))
                m_ring.emptied(nc.vector.scalar_tensor_tensor(out=slot[:], in0=rank, scalar=1.0, in1=kept[:],
                                                         op0=ALU.add, op1=ALU.mult), job)
                m_ring.wait_emptied(dve, job)

            def onehots(e):
                if e >= EG:
                    m_ring.wait(dve, ("slots", GROUP_OF[e - EG]))
                for t in range(NT):
                    ins = nc.vector.tensor_scalar(onehot[:, e % EG, t, :], slot_iota[:], slot[:, t, e:e + 1],
                                                  None, ALU.is_equal)
                ins.then_inc(onehot_ready, 1)

            def tokens_of_slots(g):
                job, n = ("slots", g), len(SLOT_GROUPS[g])
                first = SLOT_GROUPS[g][0]
                m_ring.wait(dve, job)
                if g >= 1:
                    dve.wait_ge(tok_ready, g)
                m_ring.emptied(nc.vector.tensor_copy(slot_vals[:, 0:n].rearrange("p e v -> p (e v)"),
                                                     m_ring.bank(job)[:, 0:6 * n]), job)
                m_ring.wait_emptied(dve, job)
                link(nc.vector.tensor_tensor(tok_f[:, 0:n], slot_vals[:, 0:n, 0], slot_vals[:, 0:n, 1], ALU.add))
                link(nc.vector.tensor_scalar(empty[:, 0:n], slot_vals[:, 0:n, 2], -1.0, 1.0, ALU.mult, ALU.add))
                link(nc.vector.tensor_reduce(slot_w[:, first:first + n], slot_vals[:, 0:n, 3:6], AX.X, ALU.add))
                nc.vector.scalar_tensor_tensor(out=tok_i[:, first:first + n], in0=empty[:, 0:n],
                                               scalar=spare_row[:, 0:1], in1=tok_f[:, 0:n],
                                               op0=ALU.mult, op1=ALU.add).then_inc(tok_ready, 1)

            def expert_mid(e):
                job = ("up", e)
                n = GU[job]
                dve.wait_ge(act_ready, n + 1)
                if e >= 2:
                    o_ring.wait(dve, ("turn", e - 2))
                s_ring.emptied(nc.vector.tensor_tensor(e_mid[:, e % 2], s_ring.bank(job)[:, I:2 * I],
                                                       e_act[:, n % 2, :], ALU.mult), job)

            def expert_out(e):
                job = ("down", e)
                m_ring.wait(dve, job)
                if e >= 3:
                    dve.wait_ge(scattered, 16 * (e - 2))
                m_ring.emptied(nc.vector.tensor_scalar(y_rows[:, e % 3, :], m_ring.bank(job)[:, 0:H],
                                                       slot_w[:, e:e + 1], None, ALU.mult), job)

            for b in range(B):
                dve.wait_ge(x_in[b], 16)
                norm_stats(xs, b, stats, mv, var_ready)
                if b == 0:
                    normalise(0)
                    split(0, 0, "k")
            split(0, 1, "q")
            for b in (1, 2):
                normalise(b)
                split(b, 0, "k")
                split(b, 1, "q")
            for u in range(NS):
                maxima(0, u)
            shift_parts(0)
            normalise(3)
            split(3, 0, "k")
            split(3, 1, "q")
            for b in range(B):
                for g in range(NG):
                    if b + 1 < B:
                        for u in range(3):
                            maxima(b + 1, 3 * g + u)
                    if g == 0 and b >= 1:
                        normalise2(b - 1)
                    if g == 1 and b >= 1:
                        copy_logits(b - 1)
                if b + 1 < B:
                    shift_parts(b + 1)
                attention_out(b, 0)
                attention_out(b, 1)
                fill = SHARED_FILL.get(b, ((), (), ()))
                for stage in range(3):
                    if stage == 2:
                        add_residual(b)
                    if stage == 2 and b == B - 1:
                        normalise2(b)
                    for job in fill[stage]:
                        if job[0] == "gu":
                            gu_mid(*job[1:])
                        else:
                            shared_out(*job[1:])
            copy_logits(B - 1)
            gu_mid(2, 2)
            route_start()
            shared_out(2)
            gu_mid(3, 0)
            route_weights()
            gu_mid(3, 1)
            slots_of_tokens()
            for e in SLOT_GROUPS[0]:
                onehots(e)
            gu_mid(3, 2)
            tokens_of_slots(0)
            for e in SLOT_GROUPS[1]:
                onehots(e)
            shared_out(3)
            tokens_of_slots(1)
            for e in SLOT_GROUPS[2]:
                onehots(e)
            tokens_of_slots(2)
            for e in range(E + 2):
                if e < E:
                    expert_mid(e)
                if e < E - 8:
                    onehots(e + 8)
                if e in (4, 8):
                    tokens_of_slots(EARLY_GROUPS + e // 4 - 1)
                if e >= 2:
                    expert_out(e - 2)

        @block.tensor
        def _(pe):
            def keys(b):
                if b == 0:
                    pe.wait_ge(lat_in, 16)
                    pe.wait_ge(wkv_in, 16)
                if b == 1:
                    pe.wait_ge(lat_in, 32)
                job = ("k", b)
                m_ring.begin(pe, job)
                for m in range(2):
                    last = nc.tensor.matmul(m_ring.bank(job)[:, S * m:S * m + S], wkv[:, P * m:P * m + P], lat[:, b, :],
                                            start=True, stop=True)
                m_ring.filled(last, job)

            def values(b):
                job = ("v", b)
                m_ring.begin(pe, job)
                for c in range(QT):
                    last = nc.tensor.matmul(m_ring.bank(job)[:, H * c:H * c + H], lat[:, b, P * c:P * c + P], wkv[:, H:],
                                            start=True, stop=True)
                m_ring.filled(last, job)

            def turn_x(b):
                job = ("x", b)
                pe.wait_ge(xn_ready, QT * (b + 1))
                if b == 0:
                    pe.wait_ge(consts, 2)
                m_ring.begin(pe, job)
                for c in range(HC):
                    for t in range(QT):
                        o = S * c + P * t
                        last = nc.tensor.transpose(m_ring.bank(job)[:, o:o + P], xn[:, b % 2, t, P * c:P * c + P], ident[:])
                m_ring.filled(last, job)

            def queries(b):
                m_ring.wait_emptied(pe, ("x", b))
                if b == 0:
                    pe.wait_ge(wq_in, 16)
                job = ("q", b)
                m_ring.begin(pe, job)
                for m in range(2):
                    for c in range(HC):
                        last = nc.tensor.matmul(m_ring.bank(job)[:, S * m:S * m + S], wq[:, c, P * m:P * m + P],
                                                xn_t[:, S * c:S * c + S], start=(c == 0), stop=(c == HC - 1))
                m_ring.filled(last, job)

            def scores(b, u):
                job = ("s", b, u)
                if u == 0:
                    if b == 0:
                        pe.wait_ge(consts, 5)
                    for k in "kq":
                        pe.wait_ge(rows_in[k][b % 2], 16 * 6 * (b // 2 + 1))
                s_ring.begin(pe, job)
                bank = s_ring.bank(job)
                if u < 4:
                    qt, heads, keys = 0, range(GH * u, GH * u + GH), P
                    masked = bank[:].rearrange("p (h k) -> p h k", h=GH)
                else:
                    qt, heads, keys = 1, range(2 * (u - 4), 2 * (u - 4) + 2), S
                    masked = bank[:].rearrange("p (h k) -> p h k", h=2)[:, :, P:]
                nc.tensor.matmul(masked, ident_b[:], mask_b[:].unsqueeze(1).to_broadcast([P, len(heads), P]),
                                 start=True, stop=False, skip_group_check=True)
                for j, h in enumerate(heads):
                    last = nc.tensor.matmul(bank[:, keys * j:keys * j + keys],
                                            q_rows[0:SPLIT_ROWS, b % 2, h, P * qt:P * qt + P],
                                            k_rows[0:SPLIT_ROWS, b % 2, h, 0:keys],
                                            start=False, stop=(j == len(heads) - 1), skip_group_check=True)
                s_ring.filled(last, job)

            def transpose_shift(b):
                job = ("shift", b)
                pe.wait_ge(shift_ready, b + 1)
                m_ring.begin(pe, job)
                for qt in range(QT):
                    last = nc.tensor.matmul(m_ring.bank(job)[0:3 * NH, P * qt:P * qt + P],
                                            shift[:, b % 2, qt].rearrange("p a h -> p (a h)"), ident_b[:],
                                            start=True, stop=True)
                m_ring.filled(last, job)

            def scores_t(b, g, u):
                job = ("st", b, g, u)
                if g == 0 and u == 0:
                    pe.wait_ge(shift_in[b % 2], 48 * (b // 2 + 1))
                t_ring.begin(pe, job)
                bank = t_ring.bank(job)
                k, q = k_rows[0:ROWS, b % 2], q_rows[0:ROWS, b % 2]
                if u < 2:
                    for j in range(2):
                        h = GH * g + 2 * u + j
                        last = nc.tensor.matmul(bank[:, S * j:S * j + S], k[:, h, 0:P], q[:, h, :],
                                                start=True, stop=True)
                else:
                    for j in range(GH):
                        h = GH * g + j
                        last = nc.tensor.matmul(bank[:, P * j:P * j + P], k[:, h, P:], q[:, h, P:],
                                                start=True, stop=True)
                t_ring.filled(last, job)

            def outputs(b, g):
                job = ("o", b, g)
                pe.wait_ge(probs_masked, 3 * (NG * b + g + 1))
                if g == 0:
                    m_ring.wait_emptied(pe, ("v", b))
                o_ring.begin(pe, job)
                o_ps = o_ring.bank(job)
                for j in range(GH):
                    nc.tensor.matmul(o_ps[32 * j:32 * j + 32, 0:S], v_ones[:, b, 0, GH * g + j, :],
                                     probs[:, g % 2, j // 2, S * (j % 2):S * (j % 2) + S],
                                     start=True, stop=False)
                for j in range(GH):
                    last = nc.tensor.matmul(o_ps[32 * j:32 * j + 32, P:S], v_ones[:, b, 1, GH * g + j, :],
                                            probs[:, g % 2, 2, P * j:P * j + P],
                                            start=False, stop=True)
                o_ring.filled(last, job)

            def turn_outputs(b, qt):
                job = ("ot", b, qt)
                if qt == 0:
                    o_ring.wait_emptied(pe, ("o", b, NG - 1))
                m_ring.begin(pe, job)
                for g in range(NG):
                    last = nc.tensor.transpose(m_ring.bank(job)[:, P * g:P * g + P], o_t[:, g, P * qt:P * qt + P], ident[:])
                m_ring.filled(last, job)

            def turn_attention(b):
                job = ("at", b)
                for qt in range(QT):
                    m_ring.wait_emptied(pe, ("ot", b, qt))
                m_ring.begin(pe, job)
                for c in range(HC):
                    for qt in range(QT):
                        o = S * c + P * qt
                        v = attn[:, qt].rearrange("p h d -> p (h d)")
                        last = nc.tensor.transpose(m_ring.bank(job)[:, o:o + P], v[:, P * c:P * c + P], ident[:])
                m_ring.filled(last, job)

            def project_out(b):
                m_ring.wait_emptied(pe, ("at", b))
                if b == 0:
                    pe.wait_ge(wo_in, 16)
                job = ("wo", b)
                m_ring.begin(pe, job)
                for qt in range(QT):
                    for c in range(HC):
                        last = nc.tensor.matmul(m_ring.bank(job)[:, H * qt:H * qt + H],
                                                attn_t[:, S * c + P * qt:S * c + P * qt + P],
                                                wo[:, c, :], start=(c == 0), stop=(c == HC - 1))
                m_ring.filled(last, job)

            def turn_x2(b):
                pe.wait_ge(xn2_ready, b + 1)
                job = ("x2", b)
                m_ring.begin(pe, job)
                for c in range(HC):
                    for t in range(QT):
                        o = S * c + P * t
                        last = nc.tensor.transpose(m_ring.bank(job)[:, o:o + P], xn2[:, b % 2, t, P * c:P * c + P], ident[:])
                m_ring.filled(last, job)

            def router(b):
                m_ring.wait_emptied(pe, ("x2", b))
                if b == 0:
                    pe.wait_ge(gate_in, 16)
                job = ("logits", b)
                m_ring.begin(pe, job)
                for t in range(QT):
                    for c in range(HC):
                        o = S * b + P * t
                        last = nc.tensor.matmul(m_ring.bank(job)[:, E * t:E * t + E], xn2_t[:, c, o:o + P], gate[:, c, :],
                                                start=(c == 0), stop=(c == HC - 1))
                m_ring.filled(last, job)

            def shared_up(b, c):
                if b == 0:
                    pe.wait_ge(sw_in, 48)
                job, (at, size) = ("gu", b, c), SC[c]
                s_ring.begin(pe, job)
                for half in range(2):
                    for hc in range(HC):
                        last = nc.tensor.matmul(s_ring.bank(job)[0:size, S * half:S * half + S],
                                                sgu[:, hc, half, at:at + size], xn2_t[:, hc, S * b:S * b + S],
                                                start=(hc == 0), stop=(hc == HC - 1))
                s_ring.filled(last, job)

            def shared_down(b):
                job = ("shared", b)
                for c in range(len(SC)):
                    s_ring.wait_emptied(pe, ("gu", b, c))
                m_ring.begin(pe, job)
                for qt in range(QT):
                    for c, (_, size) in enumerate(SC):
                        last = nc.tensor.matmul(m_ring.bank(job)[:, H * qt:H * qt + H],
                                                s_mid[0:size, c, P * qt:P * qt + P], sdn[0:size, c, :],
                                                start=(c == 0), stop=(c == len(SC) - 1))
                m_ring.filled(last, job)

            def ranks():
                job = ("rank",)
                pe.wait_ge(chosen_ready, 1)
                m_ring.begin(pe, job)
                v = m_ring.bank(job)[:, 0:NT * E].rearrange("p (t e) -> p t e", t=NT)
                nc.tensor.matmul(v, above_b[:], chosen_b[:], start=True, stop=False, skip_group_check=True)
                for t in range(NT - 1):
                    later = NT - 1 - t
                    last = nc.tensor.matmul(v[:, t + 1:, :], ones_b[:],
                                            chosen_b[:, t, :].unsqueeze(1).to_broadcast([P, later, E]),
                                            start=False, stop=(later == 1), skip_group_check=True)
                m_ring.filled(last, job)

            def slots(g):
                job = ("slots", g)
                if g == 0:
                    pe.wait_ge(vals_ready, 1)
                m_ring.begin(pe, job)
                for j, e in enumerate(SLOT_GROUPS[g]):
                    pe.wait_ge(onehot_ready, e + 1)
                    for t in range(NT):
                        last = nc.tensor.matmul(m_ring.bank(job)[:, 6 * j:6 * j + 6], onehot[:, e % EG, t, :],
                                                tok_vals[:, t, e, :], start=(t == 0), stop=(t == NT - 1))
                m_ring.filled(last, job)

            def expert_in(e):
                job = ("in", e)
                pe.wait_ge(gathered[e % GATHERS], 16 * (e // GATHERS + 1))
                t_ring.begin(pe, job)
                for c in range(HC):
                    last = nc.tensor.transpose(t_ring.bank(job)[:, P * c:P * c + P],
                                               xg[e % GATHERS][:, P * c:P * c + P], ident[:])
                t_ring.filled(last, job)

            def expert_up(e):
                job = ("up", e)
                if e % EG == 0:
                    pe.wait_ge(ew_in[(e // EG) % 2], 32 * (e // EG // 2 + 1))
                t_ring.wait_emptied(pe, ("in", e))
                s_ring.begin(pe, job)
                for hc in range(HC):
                    last = nc.tensor.matmul(s_ring.bank(job)[:, 0:2 * I], xg_t[:, e % 2, hc, :],
                                            wgu[:, (e // EG) % 2, e % EG, hc].rearrange("p g i -> p (g i)"),
                                            start=(hc == 0), stop=(hc == HC - 1))
                s_ring.filled(last, job)

            def expert_turn(e):
                job = ("turn", e)
                s_ring.wait_emptied(pe, ("up", e))
                o_ring.begin(pe, job)
                for c in range(2):
                    last = nc.tensor.transpose(o_ring.bank(job)[0:IC, CAP * c:CAP * c + CAP],
                                               e_mid[:, e % 2, IC * c:IC * c + IC], ident[:])
                o_ring.filled(last, job)

            def expert_down(e):
                job = ("down", e)
                o_ring.wait_emptied(pe, ("turn", e))
                m_ring.begin(pe, job)
                for c in range(2):
                    last = nc.tensor.matmul(m_ring.bank(job)[:, 0:H], e_mid_t[:, e % 2, c, :],
                                            wdn[:, (e // EG) % 2, e % EG, c, :], start=(c == 0), stop=(c == 1))
                m_ring.filled(last, job)

            step = {"k": keys, "v": values, "x": turn_x, "q": queries, "s": scores, "shift": transpose_shift,
                    "st": scores_t, "o": outputs, "ot": turn_outputs, "at": turn_attention, "wo": project_out,
                    "x2": turn_x2, "logits": router, "gu": shared_up, "shared": shared_down, "rank": ranks,
                    "slots": slots, "in": expert_in, "up": expert_up, "turn": expert_turn, "down": expert_down}
            for job in PE_ORDER:
                step[job[0]](*job[1:])


def kernel(x, ctx_512, L0_xattn_Wq, L0_xattn_Wkv_expand, L0_xattn_Wout, L0_ffn_gate_w, L0_ffn_w_gate,
           L0_ffn_w_up, L0_ffn_w_down, L0_ffn_sw_gate, L0_ffn_sw_up, L0_ffn_sw_down):
    import numpy as np
    import concourse.bacc as bacc
    from concourse.bass_utils import run_bass_kernel_spmd

    def lay(a, *axes):
        return np.ascontiguousarray(np.asarray(a).transpose(*axes))

    gate_up = np.stack([np.asarray(L0_ffn_w_gate), np.asarray(L0_ffn_w_up)]).reshape(2, E, HC, P, I)
    down = np.asarray(L0_ffn_w_down).reshape(E, 2, IC, H)
    arrays = {
        "in_x": np.ascontiguousarray(np.asarray(x)),
        "in_ctx_t": lay(ctx_512, 0, 2, 1),
        "in_wq_t": lay(L0_xattn_Wq, 1, 0),
        "in_wkv_t": lay(L0_xattn_Wkv_expand, 1, 0),
        "in_wo_t": lay(L0_xattn_Wout, 1, 0),
        "in_gate_t": lay(L0_ffn_gate_w, 1, 0),
        "in_w_gu": lay(gate_up, 3, 1, 2, 0, 4),
        "in_w_dn": lay(down, 2, 0, 1, 3),
        "in_sw_gu": lay(np.stack([np.asarray(L0_ffn_sw_gate), np.asarray(L0_ffn_sw_up)]), 1, 0, 2),
        "in_sw_dn": np.ascontiguousarray(np.asarray(L0_ffn_sw_down)),
    }
    nc = bacc.Bacc("TRN2", target_bir_lowering=False, num_devices=1)
    args = [nc.dram_tensor(n, a.shape, mybir.dt.from_np(a.dtype), kind="ExternalInput").ap()
            for n, a in arrays.items()]
    out = nc.dram_tensor("out_0", (T + CAP, H), F32, kind="ExternalOutput").ap()
    build(nc, *args, out)
    r = run_bass_kernel_spmd(nc, [arrays], core_ids=[0])
    return r.results[0]["out_0"][0:T].reshape(B, S, H)
```

```python
from contextlib import ExitStack

import concourse.bass as bass
from concourse import mybir
from concourse.alu_op_type import AluOpType as ALU

F32 = mybir.dt.float32
BF16 = mybir.dt.bfloat16
I32 = mybir.dt.int32
ACT = mybir.ActivationFunctionType
AX = mybir.AxisListType

P = 128
B, S, H = 4, 256, 256
NT = B * S // P
NH, HD = 16, 16
L = 64
HC = H // P
QT = S // P
GH = 4
NG = NH // GH
E, TOPK, I = 16, 4, 176
IC = 88
IS = 352
SC = ((0, 128), (128, 128), (256, 96))
CAP = 128
T = B * S
EG = 4
EPS = 1e-5
RSQRT_MAGIC = 0x5F3759DF
FLOOR = -87.33
MARK, TAKEN = 1.0, 2.0
NEG = -(2.0 ** 127)

Q_PARTS = ((0, 3), (1, 2), (2, 1))
K_PARTS = ((0, 1, 2), (0, 1), (0,))
SPLIT_ROWS = 6 * HD
SHIFT_ROWS = 3
ROWS = SPLIT_ROWS + SHIFT_ROWS


PAIRS = E // 2
HOTS = 4
LEAD = 6
TAIL_FILL = (
    ((("x", 3), ("v", 3)), (), (("k", 3), ("q", 3)), (), ()),
    ((("gate", 0, 0),), (("gu", 0, 0),), (("gate", 0, 1), ("gu", 0, 1)), (("gate", 0, 2),), (("gu", 0, 2),)),
    ((("half", 0),), (("shared", 0),), (("gate", 1, 0), ("gu", 1, 0)), (("gate", 1, 1),), (("gu", 1, 1),)),
    ((("gate", 1, 2),), (("gu", 1, 2),), (("half", 1),), (("shared", 1),),
     (("gate", 2, 0), ("gu", 2, 0), ("gate", 2, 1), ("gu", 2, 1), ("gate", 2, 2))),
)
KEEP_BUSY = {("k", 0): 6, ("q", 0): 4, ("k", 1): 0, ("x", 1): 2, ("q", 1): 4, ("s", 0, 0): 10, ("shift", 0): 9,
             ("in", 0): 6}
TANH_UNITS = [job for fill in TAIL_FILL[1:3] for jobs in fill for job in jobs if job[0] == "gu"]


def pe_order():
    steps = []

    def proj(b):
        steps.extend([("k", b), ("x", b), ("q", b), ("v", b)])

    proj(0)
    proj(1)
    for u in range(3 * NG):
        steps.append(("s", 0, u))
        if u in (1, 4, 7):
            steps.append(({1: "x", 4: "k", 7: "v"}[u], 2))
    steps.extend([("shift", 0), ("q", 2)])
    for b in range(B):
        for g in range(NG):
            for u in range(3):
                steps.append(("st", b, g, u))
                if b + 1 < B:
                    steps.append(("s", b + 1, 3 * g + u))
                if b >= 1 and (g, u) == (2, 2):
                    steps.append(("x2", b - 1))
                if b >= 1 and (g, u) == (3, 1):
                    steps.append(("logits", b - 1))
            if g >= 1:
                steps.append(("o", b, g - 1))
        fill = TAIL_FILL[b]
        steps.extend([*fill[0], ("o", b, NG - 1)])
        if b + 1 < B:
            steps.append(("shift", b + 1))
        steps.extend([*fill[1], ("ot", b, 0), ("ot", b, 1), *fill[2], ("at", b), *fill[3], ("wo", b), *fill[4]])
    steps.extend([("x2", B - 1), ("gu", 2, 2), ("logits", B - 1), ("half", 2), ("shared", 2), ("rank",),
                  ("gate", 3, 0), ("gu", 3, 0), ("gate", 3, 1), ("gu", 3, 1), ("rows", 0),
                  ("gate", 3, 2), ("gu", 3, 2), ("rows", 1), ("half", 3), ("shared", 3), ("in", 0), ("in", 1),
                  ("weights", 0), ("weights", 1)])
    for e in range(E + 2):
        if e < E:
            steps.append(("up", e))
        if e % 2 == 0 and e + HOTS < E:
            steps.append(("slots", (e + HOTS) // 2))
        if 1 <= e <= E:
            steps.append(("turn", e - 1))
        if e + 2 < E:
            steps.append(("in", e + 2))
        if e >= 2:
            steps.append(("down", e - 2))
    return steps


PE_ORDER = pe_order()


class Ring:

    def __init__(self, ctx, nc, name, banks, kinds):
        self.banks = [ctx.enter_context(nc.psum_tensor(f"{name}_ps{i}", [P, 512], F32)) for i in range(banks)]
        self.ready = [ctx.enter_context(nc.semaphore(f"{name}_ready{i}")) for i in range(banks)]
        self.free = [ctx.enter_context(nc.semaphore(f"{name}_free{i}")) for i in range(banks)]
        self.idle_product = None
        self.at = {}
        for job in PE_ORDER:
            if job[0] in kinds:
                n = len(self.at)
                self.at[job] = n % banks, n // banks

    def bank(self, job):
        return self.banks[self.at[job][0]]

    def begin(self, pe, job):
        i, turn = self.at[job]
        if turn:
            pe.wait_ge(self.free[i], turn)
        for _ in range(KEEP_BUSY.get(job, 0)):
            self.idle_product(self.banks[i])

    def filled(self, ins, job):
        ins.then_inc(self.ready[self.at[job][0]], 1)

    def wait(self, eng, job):
        i, turn = self.at[job]
        eng.wait_ge(self.ready[i], turn + 1)

    def emptied(self, ins, job):
        ins.then_inc(self.free[self.at[job][0]], 1)

    def wait_emptied(self, eng, job):
        i, turn = self.at[job]
        eng.wait_ge(self.free[i], turn + 1)


def build(nc, x, ctx_t, wq_t, wkv_t, wo_t, gate_t, w_gu, w_dn, sw_gu, sw_dn, out):
    q_parts_d = nc.dram_tensor("q_parts_d", [B, 3, H, S], BF16, kind="Internal").ap()
    k_parts_d = nc.dram_tensor("k_parts_d", [B, 3, H, S], BF16, kind="Internal").ap()
    xn2_d = nc.dram_tensor("xn2_d", [T + CAP, H], F32, kind="Internal").ap()
    odd_d = nc.dram_tensor("odd_d", [T + CAP, H], F32, kind="Internal").ap()

    with ExitStack() as ctx:
        def sb(name, shape, dt=F32):
            return ctx.enter_context(nc.sbuf_tensor(name, shape, dt))

        def sem(name):
            return ctx.enter_context(nc.semaphore(name))

        ident = sb("ident", [P, P])
        ident_b = sb("ident_b", [P, P], BF16)
        above_b = sb("above_b", [P, P], BF16)
        ones_b = sb("ones_b", [P, P], BF16)
        mask_b = sb("mask_b", [P, P], BF16)
        slot_iota = sb("slot_iota", [P, CAP, NT], BF16)
        cst = sb("cst", [P, P])
        spare_row = sb("spare_row", [P, 1])
        minus_slot = sb("minus_slot", [P, 1])
        eps = sb("eps", [P, 1])
        zero_rows = sb("zero_rows", [P, H])
        wq = sb("wq", [P, HC, H])
        wkv = sb("wkv", [L, 2 * H])
        wo = sb("wo", [P, HC, H])
        gate = sb("gate", [P, HC, E])
        sgu = sb("sgu", [P, HC, 2, IS])
        sdn = sb("sdn", [P, 3, H])
        wgu_early = sb("wgu_early", [P, 2, EG, HC, 2, I])
        wdn_early = sb("wdn_early", [IC, 2, EG, 2, H])
        lat = sb("lat", [L, B, S])
        xs = sb("xs", [P, NT, H])
        xn = sb("xn", [P, 2, QT, H])
        xn_t = sb("xn_t", [P, HC * S])
        stats = sb("stats", [P, NT, 6])
        mv = sb("mv", [P, NT, 2])
        std = sb("std", [P, NT])
        rstd = sb("rstd", [P, NT])
        parts = {k: sb(f"{k}_parts", [P, 2, 3, 2 * S], BF16) for k in "kq"}
        rest = sb("rest", [P, 2, 2 * S])
        q_rows = sb("q_rows", [P, 2, NH, S], BF16)
        k_rows = sb("k_rows", [P, 2, NH, S], BF16)
        v_ones = sb("v_ones", [P, B, QT, NH, 2 * HD])
        top = sb("top", [P, 2, QT, NH])
        shift = sb("shift", [P, 2, QT, 3, NH], BF16)
        shift_rest = sb("shift_rest", [P, QT, NH])
        shift_t = sb("shift_t", [3 * NH, 2, S], BF16)
        probs = sb("probs", [P, 2, 3, 2 * S])
        o_t = sb("o_t", [P, NG, S])
        den = sb("den", [P, QT, NH])
        attn = sb("attn", [P, QT, NH, HD])
        attn_t = sb("attn_t", [P, HC * S])
        stats2 = sb("stats2", [P, NT, 6])
        mv2 = sb("mv2", [P, NT, 2])
        var_eps = sb("var_eps", [P, NT])
        half_var = sb("half_var", [P, NT])
        newton = sb("newton", [P, NT])
        rstd2 = sb("rstd2", [P, NT])
        xn2 = sb("xn2", [P, 2, QT, H])
        xn2_t = sb("xn2_t", [P, HC, T])
        logits = sb("logits", [P, NT, E])
        score = sb("score", [P, NT, E])
        r1 = sb("r1", [P, NT])
        r2 = sb("r2", [P, NT])
        best = sb("best", [P, NT, 8])
        z = sb("z", [P, NT, E])
        key = sb("key", [P, NT, E + TOPK])
        four = sb("four", [P, NT, 2 * TOPK])
        chosen = sb("chosen", [P, NT, E], BF16)
        weight = sb("weight", [P, NT, E])
        kept = sb("kept", [P, NT, E])
        slot = sb("slot", [P, E, NT], BF16)
        tok_vals = sb("tok_vals", [P, NT, E, 6], BF16)
        onehot = sb("onehot", [P, HOTS, CAP, NT], BF16)
        slot_vals = sb("slot_vals", [P, 2, 6])
        own_row = sb("own_row", [P, 2])
        tok_i = sb("tok_i", [P, E], I32)
        slot_w = sb("slot_w", [P, E])
        s_act = sb("s_act", [P, 2, S])
        s_mid = sb("s_mid", [P, 3, S])
        def reuse(t, rows, *shape):
            names = "abcd"[0:len(t.shape) - 1]
            v = t[0:rows].rearrange(f"p {' '.join(names)} -> p ({' '.join(names)})")
            v = v if t.dtype == F32 else v.bitcast(F32)
            n = 1
            for k in shape:
                n *= k
            axes = "uvwx"[0:len(shape)]
            return v[:, 0:n].rearrange(f"p ({' '.join(axes)}) -> p {' '.join(axes)}", **dict(zip(axes, shape)))

        xg = [xn[:, i // QT, i % QT, :] for i in range(2 * QT)]
        xg += [reuse(parts[k], P, 6, H)[:, i] for k in "kq" for i in range(6)]
        wgu = [wgu_early[:, 0], wgu_early[:, 1], reuse(q_rows, P, EG, HC, 2, I), reuse(v_ones, P, EG, HC, 2, I)]
        wdn = [wdn_early[:, 0], wdn_early[:, 1], reuse(k_rows, IC, EG, 2, H), reuse(probs, IC, EG, 2, H)]
        xg_t = sb("xg_t", [P, 2, HC, CAP])
        e_act = sb("e_act", [P, 2, I])
        e_mid = sb("e_mid", [P, 2, I])
        e_mid_t = sb("e_mid_t", [IC, 2, 2, CAP])
        y_rows = sb("y_rows", [P, 3, H])

        s_ring = Ring(ctx, nc, "s", 2, ("s", "gu", "up"))
        t_ring = Ring(ctx, nc, "t", 2, ("st", "in"))
        o_ring = Ring(ctx, nc, "o", 1, ("o", "turn"))
        m_ring = Ring(ctx, nc, "m", 3, ("k", "v", "x", "q", "shift", "ot", "at", "wo", "x2", "logits",
                                        "shared", "rank", "rows", "weights", "slots", "down"))

        consts = sem("consts")
        pool_chain = sem("pool_chain")
        dve_chain = sem("dve_chain")
        x_in = [sem(f"x_in{b}") for b in range(B)]
        lat_in = sem("lat_in")
        wkv_in = sem("wkv_in")
        wq_in = sem("wq_in")
        wo_in = sem("wo_in")
        gate_in = sem("gate_in")
        sw_in = sem("sw_in")
        ew_in = [sem(f"ew_in{g}") for g in range(E // EG)]
        var_ready = sem("var_ready")
        std_ready = sem("std_ready")
        xn_ready = sem("xn_ready")
        lead_ready = sem("lead_ready")
        rest_ready = sem("rest_ready")
        mid_ready = sem("mid_ready")
        low_ready = sem("low_ready")
        stored = {k: [sem(f"{k}_stored{b}") for b in range(B)] for k in "kq"}
        rows_in = {k: [sem(f"{k}_rows_in{i}") for i in range(2)] for k in "kq"}
        shift_in = [sem(f"shift_in{i}") for i in range(2)]
        shift_ready = sem("shift_ready")
        probs_masked = sem("probs_masked")
        xn2_ready = sem("xn2_ready")
        xn2_stored = [sem(f"xn2_stored{i}") for i in range(2)]
        zeros_stored = sem("zeros_stored")
        z_ready = sem("z_ready")
        exp_ready = sem("exp_ready")
        chosen_ready = sem("chosen_ready")
        vals_ready = sem("vals_ready")
        onehot_ready = sem("onehot_ready")
        tok_ready = sem("tok_ready")
        act_ready = sem("act_ready")
        acc_stored = sem("acc_stored")
        gathered = [sem(f"gathered{e}") for e in range(E)]
        scattered = [sem(f"scattered{i}") for i in range(2)]
        merged = sem("merged")

        NS = 3 * NG
        GU = {job: n for n, job in enumerate(j for j in PE_ORDER if j[0] in ("gu", "up"))}
        GU_JOBS = list(GU)

        block = ctx.enter_context(nc.Block())

        @block.sync
        def _(sp):
            sp.dma_start(xs[:, 0:QT, :], x[0].rearrange("(t p) c -> p t c", p=P)).then_inc(x_in[0], 16)
            sp.dma_start(lat[:, 0, :], ctx_t[0, :, 0:S]).then_inc(lat_in, 16)
            sp.dma_start(wkv[:], wkv_t).then_inc(wkv_in, 16)
            sp.dma_start(wq[:], wq_t.rearrange("(c p) n -> p c n", p=P)).then_inc(wq_in, 16)
            sp.dma_start(xs[:, QT:2 * QT, :], x[1].rearrange("(t p) c -> p t c", p=P)).then_inc(x_in[1], 16)
            sp.dma_start(lat[:, 1:B, :], ctx_t[1:B, :, 0:S].rearrange("b l k -> l b k")).then_inc(lat_in, 16)
            for b in range(2, B):
                sp.dma_start(xs[:, QT * b:QT * b + QT, :],
                             x[b].rearrange("(t p) c -> p t c", p=P)).then_inc(x_in[b], 16)

            def store_parts(b):
                for n, (k, d) in enumerate((("k", k_parts_d), ("q", q_parts_d))):
                    sp.wait_ge(low_ready, 2 * b + n + 1)
                    sp.dma_start(d[b].rearrange("a (m p) t -> p (a m) t", p=P),
                                 parts[k][:, b % 2].rearrange("p a (m t) -> p (a m) t", m=2)
                                 ).then_inc(stored[k][b], 16)

            def load_rows(b):
                if b >= 2:
                    t_ring.wait(sp, ("st", b - 2, NG - 1, 2))
                sp.wait_ge(stored["k"][b], 16)
                src = k_parts_d[b].rearrange("a (h d) t -> a d h t", d=HD)
                row = 0
                for group in K_PARTS:
                    for part in group:
                        sp.dma_start(k_rows[row:row + HD, b % 2], src[part]).then_inc(rows_in["k"][b % 2], 16)
                        row += HD
                sp.wait_ge(stored["q"][b], 16)
                src = q_parts_d[b].rearrange("a (h d) t -> a d h t", d=HD)
                row = 0
                for part, copies in Q_PARTS:
                    for _ in range(copies):
                        sp.dma_start(q_rows[row:row + HD, b % 2], src[part]).then_inc(rows_in["q"][b % 2], 16)
                        row += HD

            def store_base(b):
                m_ring.wait_emptied(sp, ("shared", b))
                sp.dma_start(out[S * b:S * b + S].rearrange("(t p) c -> p t c", p=P),
                             xs[:, QT * b:QT * b + QT]).then_inc(acc_stored, 16)

            def load_expert(e):
                g, i = e // EG, e % EG
                sp.dma_start(wgu[g][:, i], w_gu[:, e]).then_inc(ew_in[g], 16)
                sp.dma_start(wdn[g][:, i], w_dn[:, e]).then_inc(ew_in[g], 16)

            def store_normalised(b):
                sp.wait_ge(xn2_ready, QT * (b + 1))
                sp.dma_start(xn2_d[S * b:S * b + S].rearrange("(t p) c -> p t c", p=P),
                             xn2[:, b % 2]).then_inc(xn2_stored[b % 2], 16)

            store_parts(0)
            load_rows(0)
            store_parts(1)
            load_rows(1)
            sp.dma_start(wo[:], wo_t.rearrange("(c p) n -> p c n", p=P)).then_inc(wo_in, 16)
            sp.dma_start(gate[:], gate_t.rearrange("(c p) n -> p c n", p=P)).then_inc(gate_in, 16)
            sp.dma_start(sgu[:], sw_gu.rearrange("(c p) g i -> p c g i", p=P)).then_inc(sw_in, 16)
            sp.dma_start(sdn[:, 0:2, :], sw_dn[0:2 * P].rearrange("(c p) n -> p c n", p=P)).then_inc(sw_in, 16)
            sp.dma_start(sdn[0:IS - 2 * P, 2, :], sw_dn[2 * P:IS]).then_inc(sw_in, 16)

            store_parts(2)
            for b in range(2):
                for g in range(NG):
                    t_ring.wait(sp, ("st", b, g, 2))
                    load_expert(NG * b + g)
                load_rows(b + 2)
                if b == 0:
                    store_parts(3)
                store_normalised(b)
            store_base(0)
            store_normalised(2)
            store_base(1)
            o_ring.wait(sp, ("o", B - 1, NG - 1))
            for e in range(2 * EG, 3 * EG):
                load_expert(e)
            store_normalised(3)
            for e in range(3 * EG, E):
                load_expert(e)
            store_base(2)
            store_base(3)
            sp.wait_ge(merged, 16)

        @block.gpsimd
        def _(pool):
            n_chain = [0]

            def link(ins):
                n_chain[0] += 1
                ins.then_inc(pool_chain, 1)
                pool.wait_ge(pool_chain, n_chain[0])

            n_const = [0]

            def constant(ins):
                n_const[0] += 1
                ins.then_inc(consts, 1)
                pool.wait_ge(consts, n_const[0])

            constant(nc.gpsimd.memset(eps[:], EPS))
            link(nc.gpsimd.memset(ident[:], 0.0))
            constant(nc.gpsimd.affine_select(out=ident[:], in_=ident[:], compare_op=ALU.not_equal, fill=1.0,
                                             base=0, pattern=[[-1, P]], channel_multiplier=1))
            constant(nc.gpsimd.tensor_copy(ident_b[:], ident[:]))
            link(nc.gpsimd.memset(cst[:], 0.0))
            link(nc.gpsimd.affine_select(out=cst[:], in_=cst[:], compare_op=ALU.is_ge, fill=NEG,
                                         base=0, pattern=[[-1, P]], channel_multiplier=1))
            constant(nc.gpsimd.tensor_copy(mask_b[:], cst[:]))
            link(nc.gpsimd.memset(v_ones[:, :, :, :, HD:], 1.0))
            constant(nc.gpsimd.memset(k_rows[SPLIT_ROWS:P].rearrange("r b h t -> r (b h t)").bitcast(F32),
                                      1.0 + 0x3F80 / 2 ** 23))
            constant(nc.gpsimd.memset(zero_rows[:], 0.0))

            def last_parts(b):
                for n, k in enumerate("kq"):
                    pool.wait_ge(mid_ready, 2 * b + n + 1)
                    if b == 1:
                        pool.wait_ge(low_ready, 2)
                    if b >= 2:
                        pool.wait_ge(stored[k][b - 2], 16)
                    nc.gpsimd.tensor_tensor(parts[k][:, b % 2, 2, :], rest[:, n, :], parts[k][:, b % 2, 1, :],
                                            ALU.subtract).then_inc(low_ready, 1)

            def causal(b, g):
                for u in range(3):
                    t_ring.wait_emptied(pool, ("st", b, g, u))
                    if u < 2:
                        v = probs[:, g % 2, u, :].rearrange("p (h q) -> p h q", h=2)[:, :, 0:P]
                    else:
                        v = probs[:, g % 2, u, :].rearrange("p (h q) -> p h q", h=GH)
                    nc.gpsimd.affine_select(out=v, in_=v, compare_op=ALU.is_ge, fill=0.0, base=0,
                                            pattern=[[0, v.shape[1]], [1, P]],
                                            channel_multiplier=-1).then_inc(probs_masked, 1)

            last_parts(1)
            link(nc.gpsimd.memset(cst[:], 1.0))
            link(nc.gpsimd.tensor_copy(ones_b[:], cst[:]))
            link(nc.gpsimd.affine_select(out=cst[:], in_=cst[:], compare_op=ALU.is_gt, fill=0.0,
                                         base=0, pattern=[[1, P]], channel_multiplier=-1))
            link(nc.gpsimd.tensor_copy(above_b[:], cst[:]))
            link(nc.gpsimd.iota(cst[:], pattern=[[1, P]], base=1, channel_multiplier=0,
                                allow_small_or_imprecise_dtypes=True))
            link(nc.gpsimd.tensor_copy(slot_iota[:], cst[:].unsqueeze(2).to_broadcast([P, CAP, NT])))
            link(nc.gpsimd.iota(spare_row[:], pattern=[[0, 1]], base=T, channel_multiplier=1,
                                allow_small_or_imprecise_dtypes=True))
            link(nc.gpsimd.iota(minus_slot[:], pattern=[[0, 1]], base=0, channel_multiplier=-1,
                                allow_small_or_imprecise_dtypes=True))
            link(nc.gpsimd.iota(cst[:], pattern=[[0, P]], base=0, channel_multiplier=1,
                                allow_small_or_imprecise_dtypes=True))
            v = cst[:].rearrange("p (t e) -> p t e", t=NT)
            link(nc.gpsimd.tensor_copy(tok_vals[:, :, :, 0], v))
            link(nc.gpsimd.iota(v, pattern=[[P, NT], [0, E]], base=-T, channel_multiplier=0,
                                allow_small_or_imprecise_dtypes=True))
            link(nc.gpsimd.tensor_copy(tok_vals[:, :, :, 1], v))
            link(nc.gpsimd.memset(cst[:], 1.0))
            link(nc.gpsimd.tensor_copy(tok_vals[:, :, :, 2], v))
            link(nc.gpsimd.memset(key[:], MARK))
            constant(nc.gpsimd.memset(four[:], MARK))
            for b in range(B):
                if b == 0:
                    last_parts(2)
                if b == 1:
                    pool.dma_start(xn2_d[T:T + CAP], zero_rows[:]).then_inc(zeros_stored, 16)
                    pool.dma_start(out[T:T + CAP], zero_rows[:]).then_inc(zeros_stored, 16)
                    pool.dma_start(odd_d.rearrange("(t p) c -> p t c", p=P),
                                   zero_rows[:].unsqueeze(1).to_broadcast([P, (T + CAP) // P, H])).then_inc(zeros_stored, 16)
                for g in range(NG):
                    causal(b, g)
                if b == 0:
                    last_parts(3)

            def gather(e):
                if e == 0:
                    pool.wait_ge(xn2_stored[0], 32)
                    pool.wait_ge(xn2_stored[1], 32)
                    pool.wait_ge(zeros_stored, 48)
                pool.wait_ge(tok_ready, e // 2 + 1)
                nc.gpsimd.indirect_dma_start(
                    out=xg[e], out_offset=None, in_=xn2_d[:, :],
                    in_offset=bass.IndirectOffsetOnAxis(ap=tok_i[:, e:e + 1], axis=0),
                ).then_inc(gathered[e], 16)

            def scatter(e):
                m_ring.wait_emptied(pool, ("down", e))
                if e == 0:
                    pool.wait_ge(acc_stored, 16 * B)
                if e >= 2:
                    pool.wait_ge(scattered[e % 2], 16 * (e // 2))
                nc.gpsimd.indirect_dma_start(
                    out=(odd_d if e % 2 else out)[:, :], out_offset=bass.IndirectOffsetOnAxis(ap=tok_i[:, e:e + 1], axis=0),
                    in_=y_rows[:, e % 3, :], in_offset=None, compute_op=ALU.add,
                ).then_inc(scattered[e % 2], 16)

            for e in range(LEAD):
                gather(e)
            for e in range(E):
                if e % 2 == 0 and e + LEAD < E:
                    gather(e + LEAD)
                    gather(e + LEAD + 1)
                scatter(e)
            for i in range(2):
                pool.wait_ge(scattered[i], 16 * (E // 2))
            pool.dma_start(out[0:T], odd_d[0:T], accum_op=ALU.add, max_dma_last_dim=4096).then_inc(merged, 16)

        @block.scalar
        def _(act):
            def sqrt_var(lo, hi, src, dst, done):
                nc.scalar.activation(dst[:, lo:hi], src[:, lo:hi, 1], ACT.Sqrt, bias=eps[:, 0:1]).then_inc(done, 1)

            def copy_k(b):
                m_ring.wait(act, ("k", b))
                if b >= 2:
                    act.wait_ge(stored["k"][b - 2], 16)
                nc.scalar.activation(parts["k"][:, b % 2, 0, :], m_ring.bank(("k", b))[:], ACT.Copy).then_inc(lead_ready, 1)

            def copy_v(b):
                m_ring.wait(act, ("v", b))
                m_ring.emptied(nc.scalar.activation(
                    v_ones[:, b, :, :, 0:HD],
                    m_ring.bank(("v", b))[:].rearrange("p (c h d) -> p c h d", c=QT, h=NH), ACT.Copy), ("v", b))

            def copy_x(b):
                m_ring.wait(act, ("x", b))
                if b >= 1:
                    m_ring.wait(act, ("q", b - 1))
                m_ring.emptied(nc.scalar.activation(xn_t[:], m_ring.bank(("x", b))[:], ACT.Copy), ("x", b))

            def copy_q(b):
                m_ring.wait(act, ("q", b))
                if b >= 2:
                    act.wait_ge(stored["q"][b - 2], 16)
                nc.scalar.activation(parts["q"][:, b % 2, 0, :], m_ring.bank(("q", b))[:], ACT.Copy).then_inc(lead_ready, 1)

            def exps(b, g, u):
                job = ("st", b, g, u)
                t_ring.wait(act, job)
                if NG * b + g >= 2:
                    o_ring.wait(act, ("o", b, g - 2) if g >= 2 else ("o", b - 1, g + 2))
                t_ring.emptied(nc.scalar.activation(probs[:, g % 2, u, :], t_ring.bank(job)[:], ACT.Exp,
                                                    scale=HD ** -0.5), job)

            def copy_o(b, g):
                o_ring.wait(act, ("o", b, g))
                if b >= 1 and g == 0:
                    m_ring.wait(act, ("ot", b - 1, 1))
                o_ring.emptied(nc.scalar.activation(o_t[:, g, :], o_ring.bank(("o", b, g))[:, 0:S], ACT.Copy),
                               ("o", b, g))

            def send_shift(b):
                m_ring.wait(act, ("shift", b))
                if b >= 2:
                    act.wait_ge(shift_in[b % 2], 16 * (b // 2))
                m_ring.emptied(nc.scalar.activation(shift_t[:, b % 2, :], m_ring.bank(("shift", b))[0:3 * NH, 0:S], ACT.Copy),
                          ("shift", b))
                m_ring.wait_emptied(act, ("shift", b))
                if b >= 2:
                    t_ring.wait(act, ("st", b - 2, NG - 1, 2))
                act.dma_start(q_rows[SPLIT_ROWS:ROWS, b % 2],
                              shift_t[:, b % 2, :]).then_inc(shift_in[b % 2], 16)

            def copy_at(b):
                m_ring.wait(act, ("at", b))
                if b >= 1:
                    m_ring.wait(act, ("wo", b - 1))
                m_ring.emptied(nc.scalar.activation(attn_t[:], m_ring.bank(("at", b))[:], ACT.Copy), ("at", b))

            def copy_x2(b):
                m_ring.wait(act, ("x2", b))
                m_ring.emptied(nc.scalar.activation(
                    xn2_t[:, :, S * b:S * b + S],
                    m_ring.bank(("x2", b))[:].rearrange("p (c t) -> p c t", c=HC), ACT.Copy), ("x2", b))

            def act_of(job, rows, cols, dst, func, scale):
                n = GU[job]
                s_ring.wait(act, job)
                if n >= 2:
                    s_ring.wait_emptied(act, GU_JOBS[n - 2])
                nc.scalar.activation(dst[0:rows, n % 2, :], s_ring.bank(job)[0:rows, 0:cols],
                                     func, scale=scale).then_inc(act_ready, 1)

            def gu_act(b, c):
                job = ("gu", b, c)
                if job in TANH_UNITS:
                    act_of(job, SC[c][1], S, s_act, ACT.Tanh, 0.5)
                else:
                    act_of(job, SC[c][1], S, s_act, ACT.Silu, 1.0)

            def copy_in(e):
                job = ("in", e)
                t_ring.wait(act, job)
                if e >= 2:
                    s_ring.wait(act, ("up", e - 2))
                t_ring.emptied(nc.scalar.activation(xg_t[:, e % 2].rearrange("p c s -> p (c s)"),
                                                    t_ring.bank(job)[:, 0:HC * CAP], ACT.Copy), job)

            def copy_turn(e):
                job = ("turn", e)
                o_ring.wait(act, job)
                if e >= 2:
                    m_ring.wait(act, ("down", e - 2))
                o_ring.emptied(nc.scalar.activation(e_mid_t[:, e % 2].rearrange("p c s -> p (c s)"),
                                                    o_ring.bank(job)[0:IC, 0:2 * CAP], ACT.Copy), job)

            def std_of(b):
                act.wait_ge(var_ready, b + 1)
                sqrt_var(QT * b, QT * b + QT, mv, std, std_ready)

            act.wait_ge(consts, 1)
            nc.scalar.activation(std[:, 0:1], eps[:], ACT.Sqrt).then_inc(std_ready, 1)
            act.wait_ge(std_ready, 1)
            std_of(0)
            copy_k(0)
            copy_x(0)
            copy_q(0)
            std_of(1)
            copy_v(0)
            copy_k(1)
            copy_x(1)
            std_of(2)
            std_of(3)
            copy_q(1)
            copy_v(1)
            copy_x(2)
            copy_k(2)
            copy_v(2)
            send_shift(0)
            copy_q(2)
            filling = {"x": copy_x, "k": copy_k, "q": copy_q, "v": copy_v, "gu": gu_act}

            def fill(jobs):
                for job in jobs:
                    if job[0] in filling:
                        filling[job[0]](*job[1:])

            for b in range(B):
                for g in range(NG):
                    for u in range(3):
                        exps(b, g, u)
                        if b >= 1 and (g, u) == (2, 2):
                            copy_x2(b - 1)
                    if g >= 1:
                        copy_o(b, g - 1)
                fill(TAIL_FILL[b][0])
                copy_o(b, NG - 1)
                if b + 1 < B:
                    send_shift(b + 1)
                fill(TAIL_FILL[b][1])
                fill(TAIL_FILL[b][2])
                copy_at(b)
                fill(TAIL_FILL[b][3])
                fill(TAIL_FILL[b][4])
            copy_x2(B - 1)
            gu_act(2, 2)
            act.wait_ge(z_ready, 1)
            nc.scalar.activation(score[:], z[:], ACT.Exp).then_inc(exp_ready, 1)
            for c in range(len(SC)):
                gu_act(3, c)
            copy_in(0)
            copy_in(1)
            for e in range(E + 1):
                if e < E:
                    act_of(("up", e), P, I, e_act, ACT.Silu, 1.0)
                if e >= 1:
                    copy_turn(e - 1)
                if e + 2 < E:
                    copy_in(e + 2)

        @block.vector
        def _(dve):
            n_chain = [0]

            def link(ins):
                n_chain[0] += 1
                ins.then_inc(dve_chain, 1)
                dve.wait_ge(dve_chain, n_chain[0])

            def chained(ins):
                n_chain[0] += 1
                ins.then_inc(dve_chain, 1)

            def wide(v, n):
                return v.unsqueeze(2).to_broadcast([P, v.shape[1], n])

            def norm_stats(b, st, m):
                for t in range(QT * b, QT * b + QT):
                    ins = nc.vector.bn_stats(out=st[:, t, :], in_=xs[:, t, :])
                    chained(ins)
                dve.wait_ge(dve_chain, n_chain[0])
                for t in range(QT * b, QT * b + QT):
                    ins = nc.vector.bn_aggr(out=m[:, t, :], in_=st[:, t, :])
                    if t % QT < QT - 1:
                        chained(ins)
                return ins

            def normalise(b):
                dve.wait_ge(std_ready, b + 2)
                v = slice(QT * b, QT * b + QT)
                link(nc.vector.reciprocal(rstd[:, v], std[:, v]))
                if b >= 2:
                    m_ring.wait(dve, ("x", b - 2))
                for t in range(QT):
                    k = QT * b + t
                    nc.vector.tensor_scalar(xn[:, b % 2, t, :], xs[:, k, :], mv[:, k, 0:1], rstd[:, k:k + 1],
                                            ALU.subtract, ALU.mult).then_inc(xn_ready, 1)

            def split(b, n, k):
                job = (k, b)
                dve.wait_ge(lead_ready, 2 * b + n + 1)
                if b >= 1:
                    dve.wait_ge(low_ready, 2 * (b - 1) + n + 1)
                m_ring.emptied(nc.vector.tensor_tensor(rest[:, n, :], m_ring.bank(job)[:], parts[k][:, b % 2, 0, :],
                                                  ALU.subtract), job)
                m_ring.wait_emptied(dve, job)
                nc.vector.tensor_copy(parts[k][:, b % 2, 1, :], rest[:, n, :]).then_inc(mid_ready, 1)
                if b == 0:
                    dve.wait_ge(mid_ready, 2 * b + n + 1)
                    nc.vector.tensor_tensor(parts[k][:, 0, 2, :], rest[:, n, :], parts[k][:, 0, 1, :],
                                            ALU.subtract).then_inc(low_ready, 1)

            def maxima(b, u):
                job = ("s", b, u)
                s_ring.wait(dve, job)
                if u < 4:
                    src = s_ring.bank(job)[:].rearrange("p (h k) -> p h k", h=GH)
                    dst = top[:, b % 2, 0, GH * u:GH * u + GH]
                else:
                    src = s_ring.bank(job)[:].rearrange("p (h k) -> p h k", h=2)
                    dst = top[:, b % 2, 1, 2 * (u - 4):2 * (u - 4) + 2]
                s_ring.emptied(nc.vector.tensor_reduce(dst, src, AX.X, ALU.max), job)

            def shift_parts(b):
                for u in (NS - 2, NS - 1):
                    s_ring.wait_emptied(dve, ("s", b, u))
                m, sh = top[:, b % 2], shift[:, b % 2]
                if b >= 2:
                    m_ring.wait(dve, ("shift", b - 2))
                link(nc.vector.tensor_scalar(sh[:, :, 0, :], m, -1.0, None, ALU.mult))
                link(nc.vector.scalar_tensor_tensor(out=shift_rest[:], in0=m, scalar=-1.0, in1=sh[:, :, 0, :],
                                                    op0=ALU.mult, op1=ALU.subtract))
                link(nc.vector.tensor_copy(sh[:, :, 1, :], shift_rest[:]))
                nc.vector.tensor_tensor(sh[:, :, 2, :], shift_rest[:], sh[:, :, 1, :],
                                        ALU.subtract).then_inc(shift_ready, 1)

            def attention_out(b, qt):
                job = ("ot", b, qt)
                m_ring.wait(dve, job)
                v = m_ring.bank(job)[:].rearrange("p (h r) -> p h r", h=NH)
                link(nc.vector.reciprocal(den[:, qt, :], v[:, :, HD]))
                if b >= 1:
                    m_ring.wait(dve, ("at", b - 1))
                m_ring.emptied(nc.vector.tensor_tensor(attn[:, qt], v[:, :, 0:HD], wide(den[:, qt, :], HD), ALU.mult), job)

            def add_residual(b):
                job = ("wo", b)
                m_ring.wait(dve, job)
                v = xs[:, QT * b:QT * b + QT, :]
                m_ring.emptied(nc.vector.tensor_tensor(v, m_ring.bank(job)[:].rearrange("p (t c) -> p t c", t=QT), v, ALU.add), job)
                m_ring.wait_emptied(dve, job)
                chained(norm_stats(b, stats2, mv2))

            def rsqrt_guess(b):
                v = slice(QT * b, QT * b + QT)
                dve.wait_ge(dve_chain, n_chain[0])
                chained(nc.vector.tensor_scalar(var_eps[:, v], mv2[:, v, 1], EPS, None, ALU.add))
                link(nc.vector.tensor_scalar(half_var[:, v], mv2[:, v, 1], -0.5, -0.5 * EPS, ALU.mult, ALU.add))
                chained(nc.vector.tensor_scalar(rstd2[:, v].bitcast(I32), var_eps[:, v].bitcast(I32),
                                                -0.5, float(RSQRT_MAGIC), ALU.mult, ALU.add))

            def rsqrt_step(b):
                v = slice(QT * b, QT * b + QT)
                dve.wait_ge(dve_chain, n_chain[0])
                for t in range(QT * b, QT * b + QT):
                    chained(nc.vector.scalar_tensor_tensor(out=newton[:, t:t + 1], in0=rstd2[:, t:t + 1],
                                                           scalar=half_var[:, t:t + 1], in1=rstd2[:, t:t + 1],
                                                           op0=ALU.mult, op1=ALU.mult))
                dve.wait_ge(dve_chain, n_chain[0])
                chained(nc.vector.scalar_tensor_tensor(out=rstd2[:, v], in0=newton[:, v], scalar=1.5,
                                                       in1=rstd2[:, v], op0=ALU.add, op1=ALU.mult))

            def normalise2(b):
                dve.wait_ge(dve_chain, n_chain[0])
                if b >= 2:
                    dve.wait_ge(xn2_stored[b % 2], 16 * (b // 2))
                    m_ring.wait(dve, ("x2", b - 2))
                for t in range(QT):
                    k = QT * b + t
                    nc.vector.tensor_scalar(xn2[:, b % 2, t, :], xs[:, k, :], mv2[:, k, 0:1],
                                            rstd2[:, k:k + 1], ALU.subtract, ALU.mult).then_inc(xn2_ready, 1)

            def copy_logits(b):
                job = ("logits", b)
                m_ring.wait(dve, job)
                m_ring.emptied(nc.vector.tensor_copy(logits[:, QT * b:QT * b + QT, :],
                                                m_ring.bank(job)[:, 0:QT * E].rearrange("p (t e) -> p t e", t=QT)), job)

            def gu_mid(b, c):
                job, size = ("gu", b, c), SC[c][1]
                n = GU[job]
                dve.wait_ge(act_ready, n + 1)
                if b >= 1 and c == 0:
                    m_ring.wait(dve, ("shared", b - 1))
                a, v = s_act[0:size, n % 2, :], s_ring.bank(job)
                if job in TANH_UNITS:
                    link(nc.vector.scalar_tensor_tensor(out=a, in0=a, scalar=1.0, in1=v[0:size, 0:S],
                                                        op0=ALU.add, op1=ALU.mult))
                s_ring.emptied(nc.vector.scalar_tensor_tensor(out=s_mid[0:size, c, :], in0=a,
                                                              scalar=0.5 if job in TANH_UNITS else 1.0,
                                                              in1=v[0:size, S:2 * S], op0=ALU.mult, op1=ALU.mult), job)

            def shared_out(b):
                job = ("shared", b)
                m_ring.wait(dve, job)
                v = xs[:, QT * b:QT * b + QT, :]
                m_ring.emptied(nc.vector.tensor_tensor(v, m_ring.bank(job)[:].rearrange("p (t c) -> p t c", t=QT), v, ALU.add),
                               job)

            def route_start():
                for b in range(B):
                    m_ring.wait_emptied(dve, ("logits", b))
                for t in range(NT):
                    ins = nc.vector.max(out=best[:, t, :], in_=logits[:, t, :])
                    n_chain[0] += 1
                    ins.then_inc(dve_chain, 1)
                dve.wait_ge(dve_chain, n_chain[0])
                largest = best[:, :, 0:1]
                nc.vector.tensor_tensor(z[:], logits[:], largest.to_broadcast([P, NT, E]),
                                        ALU.subtract).then_inc(z_ready, 1)
                link(nc.vector.tensor_tensor(four[:, :, 0:TOPK], best[:, :, 0:TOPK],
                                             largest.to_broadcast([P, NT, TOPK]), ALU.subtract))
                dve.wait_ge(consts, 7)
                dve.wait_ge(z_ready, 1)
                n_chain[0] += 1
                nc.vector.tensor_scalar(key[:, :, 0:E], z[:], FLOOR, None, ALU.max).then_inc(dve_chain, 1)
                link(nc.vector.tensor_scalar(four[:, :, 0:TOPK], four[:, :, 0:TOPK], FLOOR, None, ALU.max))
                for t in range(NT):
                    ins = nc.vector.match_replace(out=key[:, t, :], in_to_replace=four[:, t, :],
                                                  in_values=key[:, t, :], imm_value=TAKEN)
                    n_chain[0] += 1
                    ins.then_inc(dve_chain, 1)
                dve.wait_ge(dve_chain, n_chain[0])
                nc.vector.tensor_scalar(chosen[:], key[:, :, 0:E], TAKEN, None, ALU.is_equal).then_inc(chosen_ready, 1)

            def route_weights():
                dve.wait_ge(exp_ready, 1)
                dve.wait_ge(chosen_ready, 1)
                n_chain[0] += 1
                nc.vector.tensor_reduce(r1[:], score[:], AX.X, ALU.add).then_inc(dve_chain, 1)
                link(nc.vector.tensor_tensor(weight[:], score[:], chosen[:], ALU.mult))
                link(nc.vector.tensor_reduce(r2[:], weight[:], AX.X, ALU.add))
                link(nc.vector.scalar_tensor_tensor(out=r1[:], in0=r1[:], scalar=1e-20, in1=r2[:],
                                                    op0=ALU.mult, op1=ALU.add))
                link(nc.vector.reciprocal(r2[:], r1[:]))
                link(nc.vector.tensor_tensor(weight[:], weight[:], wide(r2[:], E), ALU.mult))
                link(nc.vector.tensor_copy(tok_vals[:, :, :, 3], weight[:]))
                link(nc.vector.tensor_tensor(weight[:], weight[:], tok_vals[:, :, :, 3], ALU.subtract))
                link(nc.vector.tensor_copy(tok_vals[:, :, :, 4], weight[:]))
                nc.vector.tensor_tensor(tok_vals[:, :, :, 5], weight[:], tok_vals[:, :, :, 4],
                                        ALU.subtract).then_inc(vals_ready, 1)

            def slots_of_tokens():
                job = ("rank",)
                m_ring.wait(dve, job)
                rank = m_ring.bank(job)[:, 0:NT * E].rearrange("p (t e) -> p t e", t=NT)
                link(nc.vector.scalar_tensor_tensor(out=kept[:], in0=rank, scalar=float(CAP), in1=chosen[:],
                                                    op0=ALU.is_lt, op1=ALU.mult))
                m_ring.emptied(nc.vector.scalar_tensor_tensor(out=slot[:].rearrange("p e t -> p t e"), in0=rank, scalar=1.0, in1=kept[:],
                                                         op0=ALU.add, op1=ALU.mult), job)
                m_ring.wait_emptied(dve, job)

            def onehots(e):
                if e >= HOTS:
                    g = (e - HOTS) // 2
                    m_ring.wait(dve, ("weights" if g < 2 else "slots", g))
                nc.vector.tensor_tensor(onehot[:, e % HOTS], slot_iota[:],
                                        slot[:, e, :].unsqueeze(1).to_broadcast([P, CAP, NT]),
                                        ALU.is_equal).then_inc(onehot_ready, 1)

            def values_of_slots(job, n):
                m_ring.wait(dve, job)
                m_ring.emptied(nc.vector.tensor_copy(slot_vals[:, :, 0:n],
                                                     m_ring.bank(job)[:, 0:2 * n].rearrange("p (e v) -> p e v", e=2)), job)
                m_ring.wait_emptied(dve, job)

            def rows_of_slots(g):
                link(nc.vector.scalar_tensor_tensor(out=own_row[:], in0=slot_vals[:, :, 2], scalar=minus_slot[:, 0:1],
                                                    in1=slot_vals[:, :, 0], op0=ALU.mult, op1=ALU.add))
                nc.vector.scalar_tensor_tensor(out=tok_i[:, 2 * g:2 * g + 2], in0=own_row[:],
                                               scalar=spare_row[:, 0:1], in1=slot_vals[:, :, 1],
                                               op0=ALU.add, op1=ALU.add).then_inc(tok_ready, 1)
                dve.wait_ge(tok_ready, g + 1)

            def early_weights(g):
                job = ("weights", g)
                m_ring.wait(dve, job)
                m_ring.emptied(nc.vector.tensor_reduce(slot_w[:, 2 * g:2 * g + 2],
                                                       m_ring.bank(job)[:, 0:6].rearrange("p (e v) -> p e v", e=2),
                                                       AX.X, ALU.add), job)
                m_ring.wait_emptied(dve, job)

            def slots_of(g):
                values_of_slots(("slots", g), 6)
                n_chain[0] += 1
                nc.vector.tensor_reduce(slot_w[:, 2 * g:2 * g + 2], slot_vals[:, :, 3:6], AX.X,
                                        ALU.add).then_inc(dve_chain, 1)
                rows_of_slots(g)

            def expert_mid(e):
                job = ("up", e)
                n = GU[job]
                dve.wait_ge(act_ready, n + 1)
                if e >= 2:
                    o_ring.wait(dve, ("turn", e - 2))
                s_ring.emptied(nc.vector.tensor_tensor(e_mid[:, e % 2], s_ring.bank(job)[:, I:2 * I],
                                                       e_act[:, n % 2, :], ALU.mult), job)

            def expert_out(e):
                job = ("down", e)
                m_ring.wait(dve, job)
                if e >= 3:
                    dve.wait_ge(scattered[(e - 3) % 2], 16 * ((e - 3) // 2 + 1))
                m_ring.emptied(nc.vector.tensor_scalar(y_rows[:, e % 3, :], m_ring.bank(job)[:, 0:H],
                                                       slot_w[:, e:e + 1], None, ALU.mult), job)

            def stats_of(b):
                dve.wait_ge(x_in[b], 16)
                norm_stats(b, stats, mv).then_inc(var_ready, 1)

            stats_of(0)
            normalise(0)
            split(0, 0, "k")
            stats_of(1)
            split(0, 1, "q")
            normalise(1)
            stats_of(2)
            stats_of(3)
            split(1, 0, "k")
            split(1, 1, "q")
            normalise(2)
            for u in range(NS):
                maxima(0, u)
            shift_parts(0)
            split(2, 0, "k")
            normalise(3)
            split(2, 1, "q")

            def fill(jobs):
                for job in jobs:
                    if job[0] in ("k", "q"):
                        split(job[1], "kq".index(job[0]), job[0])
                    elif job[0] == "gu":
                        gu_mid(*job[1:])
                    elif job[0] == "shared":
                        shared_out(*job[1:])

            for b in range(B):
                for g in range(NG):
                    if b + 1 < B:
                        for u in range(3):
                            maxima(b + 1, 3 * g + u)
                            if b >= 1 and (g, u) == (0, 1):
                                rsqrt_guess(b - 1)
                            if b >= 1 and (g, u) in ((0, 2), (1, 0), (1, 1)):
                                rsqrt_step(b - 1)
                    elif g == 0:
                        rsqrt_guess(b - 1)
                        for _ in range(3):
                            rsqrt_step(b - 1)
                    if g == 1 and b >= 1:
                        normalise2(b - 1)
                    if g == 3 and b >= 1:
                        copy_logits(b - 1)
                if b + 1 < B:
                    shift_parts(b + 1)
                fill(TAIL_FILL[b][0])
                fill(TAIL_FILL[b][1])
                attention_out(b, 0)
                attention_out(b, 1)
                fill(TAIL_FILL[b][2])
                fill(TAIL_FILL[b][3])
                add_residual(b)
                if b == B - 1:
                    rsqrt_guess(b)
                    rsqrt_step(b)
                    gu_mid(2, 0)
                    rsqrt_step(b)
                    rsqrt_step(b)
                    normalise2(b)
                    gu_mid(2, 1)
                else:
                    fill(TAIL_FILL[b][4])
            gu_mid(2, 2)
            copy_logits(B - 1)
            route_start()
            shared_out(2)
            slots_of_tokens()
            onehots(0)
            onehots(1)
            gu_mid(3, 0)
            values_of_slots(("rows", 0), 3)
            rows_of_slots(0)
            onehots(2)
            gu_mid(3, 1)
            onehots(3)
            gu_mid(3, 2)
            values_of_slots(("rows", 1), 3)
            rows_of_slots(1)
            route_weights()
            shared_out(3)
            early_weights(0)
            early_weights(1)
            onehots(4)
            onehots(5)
            for e in range(E + 2):
                if e < E:
                    expert_mid(e)
                if e % 2 == 0 and e + HOTS < E:
                    slots_of((e + HOTS) // 2)
                if e + LEAD < E:
                    onehots(e + LEAD)
                if e >= 2:
                    expert_out(e - 2)

        @block.tensor
        def _(pe):
            def idle_product(bank):
                nc.tensor.matmul(bank[:].rearrange("p (n k) -> p n k", k=P), ident_b[:],
                                 mask_b[:].unsqueeze(1).to_broadcast([P, 4, P]),
                                 start=True, stop=True, skip_group_check=True)

            for ring in (s_ring, t_ring, m_ring):
                ring.idle_product = idle_product

            def keys(b):
                job = ("k", b)
                if b == 0:
                    pe.wait_ge(consts, 4)
                m_ring.begin(pe, job)
                if b == 0:
                    pe.wait_ge(lat_in, 16)
                    pe.wait_ge(wkv_in, 16)
                if b == 1:
                    pe.wait_ge(lat_in, 32)
                for m in range(2):
                    last = nc.tensor.matmul(m_ring.bank(job)[:, S * m:S * m + S], wkv[:, P * m:P * m + P], lat[:, b, :],
                                            start=True, stop=True)
                m_ring.filled(last, job)

            def values(b):
                job = ("v", b)
                m_ring.begin(pe, job)
                for c in range(QT):
                    last = nc.tensor.matmul(m_ring.bank(job)[:, H * c:H * c + H], lat[:, b, P * c:P * c + P], wkv[:, H:],
                                            start=True, stop=True)
                m_ring.filled(last, job)

            def turn_x(b):
                job = ("x", b)
                m_ring.begin(pe, job)
                pe.wait_ge(xn_ready, QT * (b + 1))
                for c in range(HC):
                    for t in range(QT):
                        o = S * c + P * t
                        last = nc.tensor.transpose(m_ring.bank(job)[:, o:o + P], xn[:, b % 2, t, P * c:P * c + P], ident[:])
                m_ring.filled(last, job)

            def queries(b):
                job = ("q", b)
                m_ring.begin(pe, job)
                m_ring.wait_emptied(pe, ("x", b))
                if b == 0:
                    pe.wait_ge(wq_in, 16)
                for m in range(2):
                    for c in range(HC):
                        last = nc.tensor.matmul(m_ring.bank(job)[:, S * m:S * m + S], wq[:, c, P * m:P * m + P],
                                                xn_t[:, S * c:S * c + S], start=(c == 0), stop=(c == HC - 1))
                m_ring.filled(last, job)

            def scores(b, u):
                job = ("s", b, u)
                s_ring.begin(pe, job)
                if u == 0:
                    if b == 0:
                        pe.wait_ge(consts, 5)
                    for k in "kq":
                        pe.wait_ge(rows_in[k][b % 2], 16 * 6 * (b // 2 + 1))
                bank = s_ring.bank(job)
                if u < 4:
                    qt, heads, keys = 0, range(GH * u, GH * u + GH), P
                    masked = bank[:].rearrange("p (h k) -> p h k", h=GH)
                else:
                    qt, heads, keys = 1, range(2 * (u - 4), 2 * (u - 4) + 2), S
                    masked = bank[:].rearrange("p (h k) -> p h k", h=2)[:, :, P:]
                nc.tensor.matmul(masked, ident_b[:], mask_b[:].unsqueeze(1).to_broadcast([P, len(heads), P]),
                                 start=True, stop=False, skip_group_check=True)
                for j, h in enumerate(heads):
                    last = nc.tensor.matmul(bank[:, keys * j:keys * j + keys],
                                            q_rows[0:SPLIT_ROWS, b % 2, h, P * qt:P * qt + P],
                                            k_rows[0:SPLIT_ROWS, b % 2, h, 0:keys],
                                            start=False, stop=(j == len(heads) - 1), skip_group_check=True)
                s_ring.filled(last, job)

            def transpose_shift(b):
                job = ("shift", b)
                m_ring.begin(pe, job)
                pe.wait_ge(shift_ready, b + 1)
                for qt in range(QT):
                    last = nc.tensor.matmul(m_ring.bank(job)[0:3 * NH, P * qt:P * qt + P],
                                            shift[:, b % 2, qt].rearrange("p a h -> p (a h)"), ident_b[:],
                                            start=True, stop=True)
                m_ring.filled(last, job)

            def scores_t(b, g, u):
                job = ("st", b, g, u)
                if g == 0 and u == 0:
                    pe.wait_ge(shift_in[b % 2], 16 * (b // 2 + 1))
                t_ring.begin(pe, job)
                bank = t_ring.bank(job)
                k, q = k_rows[0:ROWS, b % 2], q_rows[0:ROWS, b % 2]
                if u < 2:
                    for j in range(2):
                        h = GH * g + 2 * u + j
                        last = nc.tensor.matmul(bank[:, S * j:S * j + S], k[:, h, 0:P], q[:, h, :],
                                                start=True, stop=True)
                else:
                    for j in range(GH):
                        h = GH * g + j
                        last = nc.tensor.matmul(bank[:, P * j:P * j + P], k[:, h, P:], q[:, h, P:],
                                                start=True, stop=True)
                t_ring.filled(last, job)

            def outputs(b, g):
                job = ("o", b, g)
                pe.wait_ge(probs_masked, 3 * (NG * b + g + 1))
                if g == 0:
                    m_ring.wait_emptied(pe, ("v", b))
                o_ring.begin(pe, job)
                o_ps = o_ring.bank(job)
                for j in range(GH):
                    nc.tensor.matmul(o_ps[32 * j:32 * j + 32, 0:S], v_ones[:, b, 0, GH * g + j, :],
                                     probs[:, g % 2, j // 2, S * (j % 2):S * (j % 2) + S],
                                     start=True, stop=False)
                for j in range(GH):
                    last = nc.tensor.matmul(o_ps[32 * j:32 * j + 32, P:S], v_ones[:, b, 1, GH * g + j, :],
                                            probs[:, g % 2, 2, P * j:P * j + P],
                                            start=False, stop=True)
                o_ring.filled(last, job)

            def turn_outputs(b, qt):
                job = ("ot", b, qt)
                if qt == 0:
                    o_ring.wait_emptied(pe, ("o", b, NG - 1))
                m_ring.begin(pe, job)
                for g in range(NG):
                    last = nc.tensor.transpose(m_ring.bank(job)[:, P * g:P * g + P], o_t[:, g, P * qt:P * qt + P], ident[:])
                m_ring.filled(last, job)

            def turn_attention(b):
                job = ("at", b)
                for qt in range(QT):
                    m_ring.wait_emptied(pe, ("ot", b, qt))
                m_ring.begin(pe, job)
                for c in range(HC):
                    for qt in range(QT):
                        o = S * c + P * qt
                        v = attn[:, qt].rearrange("p h d -> p (h d)")
                        last = nc.tensor.transpose(m_ring.bank(job)[:, o:o + P], v[:, P * c:P * c + P], ident[:])
                m_ring.filled(last, job)

            def project_out(b):
                m_ring.wait_emptied(pe, ("at", b))
                if b == 0:
                    pe.wait_ge(wo_in, 16)
                job = ("wo", b)
                m_ring.begin(pe, job)
                for qt in range(QT):
                    for c in range(HC):
                        last = nc.tensor.matmul(m_ring.bank(job)[:, H * qt:H * qt + H],
                                                attn_t[:, S * c + P * qt:S * c + P * qt + P],
                                                wo[:, c, :], start=(c == 0), stop=(c == HC - 1))
                m_ring.filled(last, job)

            def turn_x2(b):
                pe.wait_ge(xn2_ready, QT * (b + 1))
                job = ("x2", b)
                m_ring.begin(pe, job)
                for c in range(HC):
                    for t in range(QT):
                        o = S * c + P * t
                        last = nc.tensor.transpose(m_ring.bank(job)[:, o:o + P], xn2[:, b % 2, t, P * c:P * c + P], ident[:])
                m_ring.filled(last, job)

            def router(b):
                m_ring.wait_emptied(pe, ("x2", b))
                if b == 0:
                    pe.wait_ge(gate_in, 16)
                job = ("logits", b)
                m_ring.begin(pe, job)
                for t in range(QT):
                    for c in range(HC):
                        o = S * b + P * t
                        last = nc.tensor.matmul(m_ring.bank(job)[:, E * t:E * t + E], xn2_t[:, c, o:o + P], gate[:, c, :],
                                                start=(c == 0), stop=(c == HC - 1))
                m_ring.filled(last, job)

            def shared_gate(b, c):
                if b == 0:
                    pe.wait_ge(sw_in, 48)
                s_ring.begin(pe, ("gu", b, c))
                return shared_product(b, c, 0)

            def shared_up(b, c):
                s_ring.filled(shared_product(b, c, 1), ("gu", b, c))

            def shared_product(b, c, half):
                at, size = SC[c]
                for hc in range(HC):
                    last = nc.tensor.matmul(s_ring.bank(("gu", b, c))[0:size, S * half:S * half + S],
                                            sgu[:, hc, half, at:at + size], xn2_t[:, hc, S * b:S * b + S],
                                            start=(hc == 0), stop=(hc == HC - 1))
                return last

            def shared_half(b):
                for c in range(len(SC)):
                    s_ring.wait_emptied(pe, ("gu", b, c))
                m_ring.begin(pe, ("shared", b))
                shared_rows(b, 0)

            def shared_down(b):
                m_ring.filled(shared_rows(b, 1), ("shared", b))

            def shared_rows(b, qt):
                for c, (_, size) in enumerate(SC):
                    last = nc.tensor.matmul(m_ring.bank(("shared", b))[:, H * qt:H * qt + H],
                                            s_mid[0:size, c, P * qt:P * qt + P], sdn[0:size, c, :],
                                            start=(c == 0), stop=(c == len(SC) - 1))
                return last

            def ranks():
                job = ("rank",)
                pe.wait_ge(chosen_ready, 1)
                m_ring.begin(pe, job)
                v = m_ring.bank(job)[:, 0:NT * E].rearrange("p (t e) -> p t e", t=NT)
                nc.tensor.matmul(v, above_b[:], chosen[:], start=True, stop=False, skip_group_check=True)
                for t in range(NT - 1):
                    later = NT - 1 - t
                    last = nc.tensor.matmul(v[:, t + 1:, :], ones_b[:],
                                            chosen[:, t, :].unsqueeze(1).to_broadcast([P, later, E]),
                                            start=False, stop=(later == 1), skip_group_check=True)
                m_ring.filled(last, job)

            def slots(job, lo, hi):
                m_ring.begin(pe, job)
                n = hi - lo
                for j, e in enumerate((2 * job[1], 2 * job[1] + 1)):
                    pe.wait_ge(onehot_ready, e + 1)
                    for t in range(NT):
                        last = nc.tensor.matmul(m_ring.bank(job)[:, n * j:n * j + n], onehot[:, e % HOTS, :, t],
                                                tok_vals[:, t, e, lo:hi], start=(t == 0), stop=(t == NT - 1))
                m_ring.filled(last, job)

            def slot_rows(g):
                slots(("rows", g), 0, 3)

            def slot_weights(g):
                if g == 0:
                    pe.wait_ge(vals_ready, 1)
                slots(("weights", g), 3, 6)

            def slot_values(g):
                slots(("slots", g), 0, 6)

            def expert_in(e):
                job = ("in", e)
                t_ring.begin(pe, job)
                pe.wait_ge(gathered[e], 16)
                for c in range(HC):
                    last = nc.tensor.transpose(t_ring.bank(job)[:, P * c:P * c + P],
                                               xg[e][:, P * c:P * c + P], ident[:])
                t_ring.filled(last, job)

            def expert_up(e):
                job = ("up", e)
                if e % EG == 0:
                    pe.wait_ge(ew_in[e // EG], 32 * EG)
                t_ring.wait_emptied(pe, ("in", e))
                s_ring.begin(pe, job)
                for hc in range(HC):
                    last = nc.tensor.matmul(s_ring.bank(job)[:, 0:2 * I], xg_t[:, e % 2, hc, :],
                                            wgu[e // EG][:, e % EG, hc].rearrange("p g i -> p (g i)"),
                                            start=(hc == 0), stop=(hc == HC - 1))
                s_ring.filled(last, job)

            def expert_turn(e):
                job = ("turn", e)
                s_ring.wait_emptied(pe, ("up", e))
                o_ring.begin(pe, job)
                for c in range(2):
                    last = nc.tensor.transpose(o_ring.bank(job)[0:IC, CAP * c:CAP * c + CAP],
                                               e_mid[:, e % 2, IC * c:IC * c + IC], ident[:])
                o_ring.filled(last, job)

            def expert_down(e):
                job = ("down", e)
                o_ring.wait_emptied(pe, ("turn", e))
                m_ring.begin(pe, job)
                for c in range(2):
                    last = nc.tensor.matmul(m_ring.bank(job)[:, 0:H], e_mid_t[:, e % 2, c, :],
                                            wdn[e // EG][:, e % EG, c, :], start=(c == 0), stop=(c == 1))
                m_ring.filled(last, job)

            step = {"k": keys, "v": values, "x": turn_x, "q": queries, "s": scores, "shift": transpose_shift,
                    "st": scores_t, "o": outputs, "ot": turn_outputs, "at": turn_attention, "wo": project_out,
                    "x2": turn_x2, "logits": router, "gate": shared_gate, "gu": shared_up, "half": shared_half, "shared": shared_down, "rank": ranks,
                    "rows": slot_rows, "weights": slot_weights, "slots": slot_values, "in": expert_in, "up": expert_up, "turn": expert_turn, "down": expert_down}
            for job in PE_ORDER:
                step[job[0]](*job[1:])


def kernel(x, ctx_512, L0_xattn_Wq, L0_xattn_Wkv_expand, L0_xattn_Wout, L0_ffn_gate_w, L0_ffn_w_gate,
           L0_ffn_w_up, L0_ffn_w_down, L0_ffn_sw_gate, L0_ffn_sw_up, L0_ffn_sw_down):
    import numpy as np
    import concourse.bacc as bacc
    from concourse.bass_utils import run_bass_kernel_spmd

    def lay(a, *axes):
        return np.ascontiguousarray(np.asarray(a).transpose(*axes))

    gate_up = np.stack([np.asarray(L0_ffn_w_gate), np.asarray(L0_ffn_w_up)]).reshape(2, E, HC, P, I)
    down = np.asarray(L0_ffn_w_down).reshape(E, 2, IC, H)
    arrays = {
        "in_x": np.ascontiguousarray(np.asarray(x)),
        "in_ctx_t": lay(ctx_512, 0, 2, 1),
        "in_wq_t": lay(L0_xattn_Wq, 1, 0),
        "in_wkv_t": lay(L0_xattn_Wkv_expand, 1, 0),
        "in_wo_t": lay(L0_xattn_Wout, 1, 0),
        "in_gate_t": lay(L0_ffn_gate_w, 1, 0),
        "in_w_gu": lay(gate_up, 3, 1, 2, 0, 4),
        "in_w_dn": lay(down, 2, 0, 1, 3),
        "in_sw_gu": lay(np.stack([np.asarray(L0_ffn_sw_gate), np.asarray(L0_ffn_sw_up)]), 1, 0, 2),
        "in_sw_dn": np.ascontiguousarray(np.asarray(L0_ffn_sw_down)),
    }
    nc = bacc.Bacc("TRN2", target_bir_lowering=False, num_devices=1)
    args = [nc.dram_tensor(n, a.shape, mybir.dt.from_np(a.dtype), kind="ExternalInput").ap()
            for n, a in arrays.items()]
    out = nc.dram_tensor("out_0", (T + CAP, H), F32, kind="ExternalOutput").ap()
    build(nc, *args, out)
    r = run_bass_kernel_spmd(nc, [arrays], core_ids=[0])
    return r.results[0]["out_0"][0:T].reshape(B, S, H)
```
